# Optimizing a Trainium2 kernel written in Bass

```python
import numpy as np
import jax
import jax.numpy as jnp

def _softmax(x, axis=-1):
    return jax.nn.softmax(x, axis=axis)

def _gelu(x):
    return jax.nn.gelu(x, approximate=True)

def _silu(x):
    return jax.nn.silu(x)

def _sigmoid(x):
    return jax.nn.sigmoid(x)

def _layernorm(x, axis=-1, eps=1e-05):
    m = jnp.mean(x, axis=axis, keepdims=True)
    v = jnp.var(x, axis=axis, keepdims=True)
    return (x - m) / jnp.sqrt(v + eps)

def _scatter_add(tgt, idx, src, axis=0):
    return tgt.at[idx].add(src)

def _segment_sum(src, seg, n):
    return jax.ops.segment_sum(src, seg, n)
kernel_name = 'mk_flamingo_gated_d1_seqx_r4_1a95cb'

def setup_inputs(seed: int=0):
    np.random.seed(seed)
    _w = jnp.asarray

    def _rec_inputs():
        import jax
        import jax.numpy as jnp
        _rk = jax.random.key(seed)
        x = -0.0003929 + 0.9999 * jax.random.normal(jax.random.fold_in(_rk, 1), (8, 100, 512), jnp.float32)
        _lenS = 100 - jax.random.randint(jax.random.fold_in(_rk, 7), (8,), 0, max(1, 100 // 4) + 1, jnp.int32)
        _lenS2 = 361 - jax.random.randint(jax.random.fold_in(_rk, 8), (8,), 0, max(1, 361 // 4) + 1, jnp.int32)
        _ctx_1024P = jax.random.normal(jax.random.fold_in(_rk, 11), (8, 16, 256), jnp.float32)
        _ctx_1024c = jax.random.dirichlet(jax.random.fold_in(_rk, 511), 0.3 * jnp.ones((16,), jnp.float32), (8, 361))
        _ctx_1024t = jnp.einsum('bsk,bkd->bsd', _ctx_1024c, _ctx_1024P)
        _ctx_1024t = _ctx_1024t * jax.lax.rsqrt(jnp.mean(jnp.square(_ctx_1024t)) + 1e-12) * 0.953939
        ctx_1024 = -0.000494167 + 1.00018 * (_ctx_1024t + 0.3 * jax.random.normal(jax.random.fold_in(_rk, 611), (8, 361, 256), jnp.float32))
        _validS = jnp.arange(100)[None, :] < _lenS[:, None]
        _validS2 = jnp.arange(361)[None, :] < _lenS2[:, None]
        _causal = jnp.tril(jnp.ones((100, 100), dtype=bool))
        mask_BxS2_bf1 = jnp.ones((8, 361), dtype=bool)
        _g = jax.random.normal(jax.random.fold_in(_rk, 9001), (2, 1), jnp.float32)
        _g = jnp.sign(_g) * jnp.maximum(jnp.abs(_g), 1.0) + (_g == 0) * 1.0
        g_xattn = _g[0]
        g_ffn = _g[1]
        return (x, ctx_1024, mask_BxS2_bf1, g_xattn, g_ffn)
    x, ctx_1024, mask_BxS2_bf1, g_xattn, g_ffn = _rec_inputs()

    def _L0_xattn_setup():
        import jax, jax.numpy as jnp
        import numpy as np
        N_HEADS = 16
        N_KV_HEADS = 8
        HEAD_DIM = 128
        D_TEXT = 512
        D_VISION = 256
        GROUPS = N_HEADS // N_KV_HEADS
        key = jax.random.key(seed)
        ks = jax.random.split(key, 6)
        B, T_text, T_vis = (4, 512, 144)
        text_hidden = jax.random.normal(ks[0], (B, T_text, D_TEXT), dtype=jnp.float32)
        vision_tokens = jax.random.normal(ks[1], (B, T_vis, D_VISION), dtype=jnp.float32)
        vision_mask = jnp.ones((B, T_vis), dtype=bool)
        s = 0.02
        Wq = jax.random.normal(ks[2], (D_TEXT, N_HEADS * HEAD_DIM), dtype=jnp.float32) * s
        Wk = jax.random.normal(ks[3], (D_VISION, N_KV_HEADS * HEAD_DIM), dtype=jnp.float32) * s
        Wv = jax.random.normal(ks[4], (D_VISION, N_KV_HEADS * HEAD_DIM), dtype=jnp.float32) * s
        Wo = jax.random.normal(ks[5], (N_HEADS * HEAD_DIM, D_TEXT), dtype=jnp.float32) * s
        return {'text_hidden': text_hidden, 'vision_tokens': vision_tokens, 'vision_mask': vision_mask, 'Wq': Wq, 'Wk': Wk, 'Wv': Wv, 'Wo': Wo}
    _L0_xattn_all = _L0_xattn_setup()
    _L0_xattn_in = {k: v for k, v in _L0_xattn_all.items() if k in ('Wq', 'Wk', 'Wv', 'Wo')}
    del _L0_xattn_all

    def _L0_ffn_setup():
        import jax, jax.numpy as jnp
        import numpy as np
        HID = 512
        N_HEADS = 16
        N_KV = 16
        HEAD_DIM = HID // N_HEADS
        N_EXP = 8
        TOP_K = 2
        MOE_I = 352
        SH_I = 1408
        EPS = 1e-06
        ROPE_THETA = 1000000.0

        def _rms(x, w):
            v = jnp.mean(jnp.square(x), axis=-1, keepdims=True)
            return x * jax.lax.rsqrt(v + EPS) * w

        def _rope(q, k):
            S, D = (q.shape[1], q.shape[-1])
            inv = 1.0 / ROPE_THETA ** (jnp.arange(0, D, 2, dtype=jnp.float32) / D)
            freqs = jnp.arange(S, dtype=jnp.float32)[:, None] * inv[None, :]
            emb = jnp.concatenate([freqs, freqs], axis=-1)
            cos = jnp.cos(emb)[None, :, None, :]
            sin = jnp.sin(emb)[None, :, None, :]

            def rot(t):
                t1, t2 = (t[..., :D // 2], t[..., D // 2:])
                return jnp.concatenate([-t2, t1], axis=-1)
            return (q * cos + rot(q) * sin, k * cos + rot(k) * sin)
        key = jax.random.key(seed)
        ks = jax.random.split(key, 20)
        s = 0.02
        d = {'x': jax.random.normal(ks[0], (2, 256, HID), jnp.float32), 'w_ln1': jnp.ones((HID,), jnp.float32), 'wq': jax.random.normal(ks[1], (HID, N_HEADS * HEAD_DIM), jnp.float32) * s, 'bq': jnp.zeros((N_HEADS * HEAD_DIM,), jnp.float32), 'wk': jax.random.normal(ks[2], (HID, N_KV * HEAD_DIM), jnp.float32) * s, 'bk': jnp.zeros((N_KV * HEAD_DIM,), jnp.float32), 'wv': jax.random.normal(ks[3], (HID, N_KV * HEAD_DIM), jnp.float32) * s, 'bv': jnp.zeros((N_KV * HEAD_DIM,), jnp.float32), 'wo': jax.random.normal(ks[4], (N_HEADS * HEAD_DIM, HID), jnp.float32) * s, 'w_ln2': jnp.ones((HID,), jnp.float32), 'w_router': jax.random.normal(ks[5], (HID, N_EXP), jnp.float32) * s, 'w_gate_e': jax.random.normal(ks[6], (N_EXP, HID, MOE_I), jnp.float32) * s, 'w_up_e': jax.random.normal(ks[7], (N_EXP, HID, MOE_I), jnp.float32) * s, 'w_down_e': jax.random.normal(ks[8], (N_EXP, MOE_I, HID), jnp.float32) * s, 'w_sh_gate': jax.random.normal(ks[9], (HID, SH_I), jnp.float32) * s, 'w_sh_up': jax.random.normal(ks[10], (HID, SH_I), jnp.float32) * s, 'w_sh_down': jax.random.normal(ks[11], (SH_I, HID), jnp.float32) * s, 'w_sh_eg': jax.random.normal(ks[12], (HID, 1), jnp.float32) * s}
        return d
    _L0_ffn_all = _L0_ffn_setup()
    _L0_ffn_in = {k: v for k, v in _L0_ffn_all.items() if k in ('w_ln1', 'wq', 'bq', 'wk', 'bk', 'wv', 'bv', 'wo', 'w_ln2', 'w_router', 'w_gate_e', 'w_up_e', 'w_down_e', 'w_sh_gate', 'w_sh_up', 'w_sh_down', 'w_sh_eg')}
    del _L0_ffn_all
    return {'x': x, 'ctx_1024': ctx_1024, 'mask_BxS2_bf1': mask_BxS2_bf1, 'g_xattn': g_xattn, 'g_ffn': g_ffn, 'L0_xattn_Wq': _L0_xattn_in['Wq'], 'L0_xattn_Wk': _L0_xattn_in['Wk'], 'L0_xattn_Wv': _L0_xattn_in['Wv'], 'L0_xattn_Wo': _L0_xattn_in['Wo'], 'L0_ffn_w_ln1': _L0_ffn_in['w_ln1'], 'L0_ffn_wq': _L0_ffn_in['wq'], 'L0_ffn_bq': _L0_ffn_in['bq'], 'L0_ffn_wk': _L0_ffn_in['wk'], 'L0_ffn_bk': _L0_ffn_in['bk'], 'L0_ffn_wv': _L0_ffn_in['wv'], 'L0_ffn_bv': _L0_ffn_in['bv'], 'L0_ffn_wo': _L0_ffn_in['wo'], 'L0_ffn_w_ln2': _L0_ffn_in['w_ln2'], 'L0_ffn_w_router': _L0_ffn_in['w_router'], 'L0_ffn_w_gate_e': _L0_ffn_in['w_gate_e'], 'L0_ffn_w_up_e': _L0_ffn_in['w_up_e'], 'L0_ffn_w_down_e': _L0_ffn_in['w_down_e'], 'L0_ffn_w_sh_gate': _L0_ffn_in['w_sh_gate'], 'L0_ffn_w_sh_up': _L0_ffn_in['w_sh_up'], 'L0_ffn_w_sh_down': _L0_ffn_in['w_sh_down'], 'L0_ffn_w_sh_eg': _L0_ffn_in['w_sh_eg']}

def reference(x, ctx_1024, mask_BxS2_bf1, g_xattn, g_ffn, L0_xattn_Wq, L0_xattn_Wk, L0_xattn_Wv, L0_xattn_Wo, L0_ffn_w_ln1, L0_ffn_wq, L0_ffn_bq, L0_ffn_wk, L0_ffn_bk, L0_ffn_wv, L0_ffn_bv, L0_ffn_wo, L0_ffn_w_ln2, L0_ffn_w_router, L0_ffn_w_gate_e, L0_ffn_w_up_e, L0_ffn_w_down_e, L0_ffn_w_sh_gate, L0_ffn_w_sh_up, L0_ffn_w_sh_down, L0_ffn_w_sh_eg):
    import jax
    import jax.numpy as jnp

    def _L0_xattn_ref(text_hidden, vision_tokens, vision_mask, Wq, Wk, Wv, Wo):
        import jax, jax.numpy as jnp
        import numpy as np
        N_HEADS = 16
        N_KV_HEADS = 8
        HEAD_DIM = 128
        D_TEXT = 512
        D_VISION = 256
        GROUPS = N_HEADS // N_KV_HEADS
        B, T_text, _ = text_hidden.shape
        T_vis = vision_tokens.shape[1]
        scale = jnp.float32(np.sqrt(HEAD_DIM))
        q = (text_hidden @ Wq).reshape(B, T_text, N_HEADS, HEAD_DIM).transpose(0, 2, 1, 3)
        k = (vision_tokens @ Wk).reshape(B, T_vis, N_KV_HEADS, HEAD_DIM).transpose(0, 2, 1, 3)
        v = (vision_tokens @ Wv).reshape(B, T_vis, N_KV_HEADS, HEAD_DIM).transpose(0, 2, 1, 3)
        k = jnp.repeat(k, GROUPS, axis=1)
        v = jnp.repeat(v, GROUPS, axis=1)
        scores = jnp.einsum('bhtd,bhsd->bhts', q, k) / scale
        mask = vision_mask[:, None, None, :]
        scores = jnp.where(mask, scores, -jnp.inf)
        attn = jax.nn.softmax(scores, axis=-1)
        attn = jnp.nan_to_num(attn, nan=0.0)
        out = jnp.einsum('bhts,bhsd->bhtd', attn, v)
        out = out.transpose(0, 2, 1, 3).reshape(B, T_text, N_HEADS * HEAD_DIM)
        return out @ Wo

    def _L0_ffn_ref(x, w_ln1, wq, bq, wk, bk, wv, bv, wo, w_ln2, w_router, w_gate_e, w_up_e, w_down_e, w_sh_gate, w_sh_up, w_sh_down, w_sh_eg):
        import jax, jax.numpy as jnp
        import numpy as np
        HID = 512
        N_HEADS = 16
        N_KV = 16
        HEAD_DIM = HID // N_HEADS
        N_EXP = 8
        TOP_K = 2
        MOE_I = 352
        SH_I = 1408
        EPS = 1e-06
        ROPE_THETA = 1000000.0

        def _rms(x, w):
            v = jnp.mean(jnp.square(x), axis=-1, keepdims=True)
            return x * jax.lax.rsqrt(v + EPS) * w

        def _rope(q, k):
            S, D = (q.shape[1], q.shape[-1])
            inv = 1.0 / ROPE_THETA ** (jnp.arange(0, D, 2, dtype=jnp.float32) / D)
            freqs = jnp.arange(S, dtype=jnp.float32)[:, None] * inv[None, :]
            emb = jnp.concatenate([freqs, freqs], axis=-1)
            cos = jnp.cos(emb)[None, :, None, :]
            sin = jnp.sin(emb)[None, :, None, :]

            def rot(t):
                t1, t2 = (t[..., :D // 2], t[..., D // 2:])
                return jnp.concatenate([-t2, t1], axis=-1)
            return (q * cos + rot(q) * sin, k * cos + rot(k) * sin)
        B, S, H = x.shape
        h = _rms(x, w_ln1)
        q = (h @ wq + bq).reshape(B, S, N_HEADS, HEAD_DIM)
        k = (h @ wk + bk).reshape(B, S, N_KV, HEAD_DIM)
        v = (h @ wv + bv).reshape(B, S, N_KV, HEAD_DIM)
        q, k = _rope(q, k)
        rep = N_HEADS // N_KV
        if rep > 1:
            k = jnp.repeat(k, rep, axis=2)
            v = jnp.repeat(v, rep, axis=2)
        scores = jnp.einsum('bqhd,bkhd->bhqk', q, k) * HEAD_DIM ** (-0.5)
        causal = jnp.tril(jnp.ones((S, S), bool))
        scores = jnp.where(causal[None, None], scores, jnp.finfo(scores.dtype).min)
        attn = jax.nn.softmax(scores, axis=-1)
        ctx = jnp.einsum('bhqk,bkhd->bqhd', attn, v).reshape(B, S, N_HEADS * HEAD_DIM)
        x = x + ctx @ wo
        h = _rms(x, w_ln2).reshape(B * S, H)
        logits = h @ w_router
        probs = jax.nn.softmax(logits, axis=-1)
        top_w, top_i = jax.lax.top_k(probs, TOP_K)
        combine = jnp.sum(jax.nn.one_hot(top_i, N_EXP, dtype=h.dtype) * top_w[..., None], axis=1)
        g = jnp.einsum('th,ehi->eti', h, w_gate_e)
        u = jnp.einsum('th,ehi->eti', h, w_up_e)
        y = jnp.einsum('eti,eih->eth', jax.nn.silu(g) * u, w_down_e)
        routed = jnp.einsum('eth,te->th', y, combine)
        sh = jax.nn.silu(h @ w_sh_gate) * (h @ w_sh_up) @ w_sh_down
        sh = sh * jax.nn.sigmoid(h @ w_sh_eg)
        x = x + (routed + sh).reshape(B, S, H)
        return x
    x = x + jnp.tanh(g_xattn[0]) * _L0_xattn_ref(_layernorm(x, axis=-1), ctx_1024, mask_BxS2_bf1, L0_xattn_Wq, L0_xattn_Wk, L0_xattn_Wv, L0_xattn_Wo)
    x = x + jnp.tanh(g_ffn[0]) * _L0_ffn_ref(_layernorm(x, axis=-1), L0_ffn_w_ln1, L0_ffn_wq, L0_ffn_bq, L0_ffn_wk, L0_ffn_bk, L0_ffn_wv, L0_ffn_bv, L0_ffn_wo, L0_ffn_w_ln2, L0_ffn_w_router, L0_ffn_w_gate_e, L0_ffn_w_up_e, L0_ffn_w_down_e, L0_ffn_w_sh_gate, L0_ffn_w_sh_up, L0_ffn_w_sh_down, L0_ffn_w_sh_eg)
    return x

_drawn_inputs = setup_inputs


def setup_inputs(seed=0):
    import zlib

    import numpy as np

    out = dict(_drawn_inputs(seed))
    spreads = {'L0_ffn_w_ln1': (1.0, 0.2),
     'L0_ffn_bq': (0.0, 0.479),
     'L0_ffn_bk': (0.0, 0.8),
     'L0_ffn_bv': (0.0, 0.1),
     'L0_ffn_w_ln2': (1.0, 0.2)}
    factors = {'L0_xattn_Wq': 6.956, 'L0_xattn_Wk': 6.616}
    for name, (base, spread) in spreads.items():
        noise = np.random.default_rng([zlib.crc32(name.encode()), seed]).standard_normal(out[name].shape)
        drawn = base * np.exp(spread * noise) if base else spread * noise
        out[name] = jnp.asarray(drawn.astype(out[name].dtype))
    for name, factor in factors.items():
        out[name] = (out[name] * factor).astype(out[name].dtype)
    return out
```

```python
from contextlib import ExitStack

import numpy as np
import concourse.bass as bass
from concourse import mybir

F = mybir.dt.float32
R = mybir.dt.float32r
BF = mybir.dt.bfloat16
U8 = mybir.dt.uint8
ALU = mybir.AluOpType
ACT = mybir.ActivationFunctionType
AX = mybir.AxisListType.X

B, T, D = 8, 100, 512
S, C = 361, 256
SP = 362
NH, NKV, HD = 16, 8, 128
FH, FD = 16, 32
NE, EI = 8, 352
HB = 4
HT = HB * T
TT = B * T
KD = D // 128
CH = [(0, 128), (128, 128), (256, S - 256)]
NJ = 11
BIG = 1.0e30
XS = float(1.0 / np.sqrt(np.float32(HD)))
FS = float(FD) ** -0.5
SWAP = [(i + 16) % 32 for i in range(32)]


class Sem:

    def __init__(self, handle):
        self.handle = handle
        self.count = 0

    def after(self, step):
        self.count += step
        return (self, self.count)


class Queue:

    def __init__(self):
        self.items = []
        self.seen = {}

    def wait(self, *tokens):
        for sem, value in tokens:
            if self.seen.get(sem, 0) < value:
                self.seen[sem] = value
                self.items.append((sem.handle, value, None))

    def do(self, emit, sem=None, step=1):
        self.items.append((sem.handle if sem else None, step, emit))
        return sem.after(step) if sem else None

    def play(self, eng):
        for handle, n, emit in self.items:
            if emit is None:
                eng.wait_ge(handle, n)
            elif handle is None:
                emit(eng)
            else:
                emit(eng).then_inc(handle, n)


class Slot:

    def __init__(self, t, sem=None):
        self.t = t
        self.sem = sem
        self.free = []


class Ring:
    def __init__(self, slots):
        self.slots = slots
        self.n = 0

    def next(self):
        self.n += 1
        return self.slots[(self.n - 1) % len(self.slots)]


def f32(ap):
    return ap.bitcast(F)


def flamingo_kernel(nc, x, ctx_in, mask, g_x, g_f, Wq, Wk, Wv, Wo, w_ln1, wq, b_q, wk, b_k, wv, b_v, wo,
                    w_ln2, w_router, w_gate, w_up, w_down, sh_gate, sh_up, sh_down, sh_eg,
                    c_id, c_causal, c_cos, c_sin, s_x1, s_x2, s_comb, out):
    top = ExitStack()
    pe, act, dve, pool, sp = Queue(), Queue(), Queue(), Queue(), Queue()
    names = {}

    def sem(name):
        if name not in names:
            names[name] = Sem(top.enter_context(nc.semaphore(name)))
        return names[name]

    def alloc(stack, name, shape, dt=F):
        return stack.enter_context(nc.sbuf_tensor(name, shape, dt))

    def matmul(o, a, b, start, stop, s=None):
        return pe.do(lambda e: e.matmul(o, a, b, start=start, stop=stop, skip_group_check=True), s)

    def mm3(o, ah, al, bh, bl, first, last, s=None, mark=None):
        matmul(o, ah, bh, first, False)
        matmul(o, ah, bl, False, False)
        return matmul(o, al, bh, False, last, s if (last if mark is None else mark) else None)

    def turn(o, i, ident, s=None):
        return pe.do(lambda e: e.transpose(o, i, ident), s)

    def activate(o, i, func, s=None, **kw):
        return act.do(lambda e: e.activation(o, i, func, **kw), s)

    def tt(q, o, a, b, op, s=None):
        return q.do(lambda e: e.tensor_tensor(o, a, b, op), s)

    def ts(q, o, a, s1, s2, op0, op1=None, s=None):
        if op1 is None:
            return q.do(lambda e: e.tensor_scalar(o, a, s1, None, op0), s)
        return q.do(lambda e: e.tensor_scalar(o, a, s1, s2, op0, op1), s)

    def stt(o, a, sc, b, op0, op1, s=None):
        return dve.do(lambda e: e.scalar_tensor_tensor(out=o, in0=a, scalar=sc, in1=b, op0=op0, op1=op1), s)

    def copy(q, o, i, s=None):
        return q.do(lambda e: e.tensor_copy(o, i), s)

    def reduce(o, i, op, s=None):
        return dve.do(lambda e: e.tensor_reduce(o, i, AX, op), s)

    def recip(o, i, s=None):
        return dve.do(lambda e: e.reciprocal(o, i), s)

    def dma(q, o, i, s):
        return q.do(lambda e: e.dma_start(o, i), s, 16)

    def dma_columns(q, o, i, s):
        return q.do(lambda e: e.dma_start(o, i, allow_slow_non_contiguous=True), s, 16)

    def split(src, hi, lo, name, ready, free=(), scale=None):
        act.wait(ready, *free)
        if scale is None:
            h = activate(hi, src, ACT.Copy, sem("act_" + name))
            dve.wait(h)
            return tt(dve, lo, src, f32(hi), ALU.subtract, sem("dve_" + name))
        h = activate(hi, src, ACT.Copy, sem("act_" + name), scale=scale)
        dve.wait(h)
        return stt(lo, src, scale, f32(hi), ALU.mult, ALU.subtract, sem("dve_" + name))

    banks = [Slot(top.enter_context(nc.psum_tensor(f"bank{i}", [128, 512], F))) for i in range(8)]

    ident = alloc(top, "ident", [128, 128])
    mask8 = alloc(top, "mask8", [T, B * S], U8)
    anyv = alloc(top, "anyv", [T, B])
    gx = alloc(top, "gx", [T, 1])
    gf = alloc(top, "gf", [T, 1])
    tgx = alloc(top, "tgx", [T, 1])
    tgf = alloc(top, "tgf", [T, 1])
    ln1c = alloc(top, "ln1c", [128, KD])
    ln2c = alloc(top, "ln2c", [128, KD])
    stat = alloc(top, "stat", [T, B, 6])
    mv = alloc(top, "mv", [T, B, 2])
    rs = alloc(top, "rs", [T, B])
    ms = alloc(top, "ms", [T, B])
    raw = Ring([Slot(alloc(top, f"raw{i}", [128, 4, 128]), sem(f"dma_raw{i}")) for i in range(4)])

    c_ident = dma(act, ident[:, :], c_id, sem("dma_ident"))
    c_mask = dma(act, mask8[:, :], bass.AP(mask.tensor, 0, [[0, T], [1, B * S]]), sem("dma_mask"))
    dma(act, gx[:, :], bass.AP(g_x.tensor, 0, [[0, T], [1, 1]]), sem("dma_small"))
    dma(act, gf[:, :], bass.AP(g_f.tensor, 0, [[0, T], [1, 1]]), sem("dma_small"))
    dma_columns(act, ln1c[:, :], w_ln1.rearrange("(k p) -> p k", p=128), sem("dma_small"))
    c_small = dma_columns(act, ln2c[:, :], w_ln2.rearrange("(k p) -> p k", p=128), sem("dma_small"))
    act.wait(c_small)
    activate(tgx[:, :], gx[:, :], ACT.Tanh, sem("act_tanh"))
    c_tanh = activate(tgf[:, :], gf[:, :], ACT.Tanh, sem("act_tanh"))
    dve.wait(c_mask)
    c_any = reduce(anyv[:, :], mask8[:, :].rearrange("p (b s) -> p b s", s=S), ALU.max, sem("dve_any"))

    def load_unit(pieces):
        r = raw.next()
        sp.wait(*r.free)
        for view, src in pieces:
            tok = dma(sp, view(r.t), src, r.sem)
        return r, tok

    def split_unit(r, tok, hi, lo, free, name="w"):
        act.wait(tok, *free)
        h = activate(hi, r.t[:, :, :], ACT.Copy, sem("act_" + name))
        pool.wait(h)
        lo_tok = tt(pool, lo, r.t[:, :, :], f32(hi), ALU.subtract, sem("pool_" + name + "l"))
        r.free = [lo_tok]
        return lo_tok

    def whole(t):
        return t[:, :, :]

    def weight_stream(ring, sources, ahead):
        waiting = []

        def fetch(src):
            r, tok = load_unit(src)
            w = ring.next()
            ready = split_unit(r, tok, w.t[:, 0, :, :], w.t[:, 1, :, :], w.free)
            waiting.append((w, ready))

        left = list(sources)
        for _ in range(min(ahead, len(left))):
            fetch(left.pop(0))
        while waiting:
            if left:
                fetch(left.pop(0))
            yield waiting.pop(0)

    def rstd(n0, n, add_square, eps, ready):
        dve.wait(ready)
        var = mv[:, n0:n0 + n, 1]
        if add_square:
            t = tt(dve, ms[:, n0:n0 + n], mv[:, n0:n0 + n, 0], mv[:, n0:n0 + n, 0], ALU.mult, sem("dve_ms"))
            dve.wait(t)
            t = stt(ms[:, n0:n0 + n], ms[:, n0:n0 + n], eps, var, ALU.add, ALU.add, sem("dve_ms"))
        else:
            t = ts(dve, ms[:, n0:n0 + n], var, eps, None, ALU.add, s=sem("dve_ms"))
        act.wait(t)
        t = activate(ms[:, n0:n0 + n], ms[:, n0:n0 + n], ACT.Sqrt, sem("act_sqrt"))
        dve.wait(t)
        return recip(rs[:, n0:n0 + n], ms[:, n0:n0 + n], sem("dve_rs"))

    def stats(rows, n0, n, ready):
        dve.wait(*ready)
        for i in range(n):
            o, a = stat[:, n0 + i, :], rows(n0 + i)
            t = dve.do(lambda e, o=o, a=a: e.bn_stats(o, a), sem("dve_bn"))
        dve.wait(t)
        for i in range(n):
            o, a = mv[:, n0 + i, :], stat[:, n0 + i, :]
            t = dve.do(lambda e, o=o, a=a: e.bn_aggr(o, a), sem("dve_bn"))
        return t

    def to_features(rows, n0, n, th, tl, col0, ready, name, scale=None):
        last = None
        for k in range(KD):
            bk = banks[k % 4]
            pe.wait(*bk.free, *ready, c_ident)
            for i in range(n):
                t = turn(bk.t[:, i * T:(i + 1) * T], rows(n0 + i)[:, k * 128:(k + 1) * 128],
                         ident[0:T, 0:T], sem("pe_turn") if i == n - 1 else None)
            last = split(bk.t[:, 0:n * T], th[:, k, col0:col0 + n * T], tl[:, k, col0:col0 + n * T],
                         name, t, scale=None if scale is None else scale[:, k:k + 1])
            bk.free = [last]
        return last

    def end_phase():
        toks = []
        for q, name in ((act, "act"), (dve, "dve"), (pool, "pool")):
            toks.append(q.do(lambda e: e.drain(), sem("phase_" + name)))
        toks.append(pe.do(lambda e: e.drain(), sem("phase_pe")))
        for q in (pe, act, dve, pool, sp):
            q.wait(*toks)

    x1 = s_x1.rearrange("b t d -> t b d")
    xin = x.rearrange("b t d -> t b d")
    done_x1 = []
    with ExitStack() as st:
        QOh = alloc(st, "QOh", [128, NH, HT], R)
        QOl = alloc(st, "QOl", [128, NH, HT], R)
        WKh = alloc(st, "WKh", [128, 2, NKV * 128], R)
        WKl = alloc(st, "WKl", [128, 2, NKV * 128], R)
        WVh = alloc(st, "WVh", [128, 2, NKV * 128], R)
        WVl = alloc(st, "WVl", [128, 2, NKV * 128], R)
        CTh = [alloc(st, f"CTh{i}", [128, 2, SP], R) for i in range(2)]
        CTl = [alloc(st, f"CTl{i}", [128, 2, SP], R) for i in range(2)]
        mb = [alloc(st, f"mb{i}", [T, S]) for i in range(2)]
        ctok = []
        wkv_ready = []
        for half in range(2):
            b0 = half * HB
            with ExitStack() as s1:
                XTh = alloc(s1, f"XTh{half}", [128, KD, HT], R)
                XTl = alloc(s1, f"XTl{half}", [128, KD, HT], R)
                X = alloc(s1, f"X{half}", [T, HB, D])
                wr = Ring([Slot(alloc(s1, f"wr{half}_{i}", [128, 2, 4, 128], R)) for i in range(3)])
                xt = dma(sp, X[:, :, :], xin[:, b0:b0 + HB, :], sem("dma_x"))
                rows = lambda i: X[:, i - b0, :]
                t = stats(rows, b0, HB, [xt])
                t = rstd(b0, HB, False, 1e-5, t)
                dve.wait(t)
                for i in range(HB):
                    t = ts(dve, X[:, i, :], X[:, i, :], mv[:, b0 + i, 0:1], rs[:, b0 + i:b0 + i + 1],
                           ALU.subtract, ALU.mult, sem("dve_norm"))
                xready = to_features(rows, b0, HB, XTh, XTl, 0, [t], "xt")
                Wqv = Wq.rearrange("(k p) n -> p k n", p=128)
                srcs = [[(whole, Wqv[:, :, n * 128:(n + 1) * 128])] for n in range(NH)]
                for n, (w, ready) in enumerate(weight_stream(wr, srcs, 2)):
                    bk = banks[4 + n % 4]
                    pe.wait(ready, xready, *bk.free)
                    for k in range(KD):
                        t = mm3(bk.t[:, 0:HT], w.t[:, 0, k, :], w.t[:, 1, k, :], XTh[:, k, :], XTl[:, k, :],
                                k == 0, k == KD - 1, sem("pe_q"))
                    w.free = [t]
                    q_ready = split(bk.t[:, 0:HT], QOh[:, n, :], QOl[:, n, :], "q", t)
                    bk.free = [q_ready]
                if half == 0:
                    for src, wh, wl in ((Wk, WKh, WKl), (Wv, WVh, WVl)):
                        v = src.rearrange("(k p) n -> p k n", p=128)
                        for c in range(4):
                            cs = slice(c * 256, (c + 1) * 256)
                            as2 = lambda t: t[:, :, :].rearrange("p a b -> p (a b)").rearrange("p (k n) -> p k n", k=2)
                            r, tok = load_unit([(as2, v[:, :, cs])])
                            act.wait(tok)
                            h = activate(wh[:, :, cs], as2(r.t), ACT.Copy, sem("act_kv"))
                            pool.wait(h)
                            wkv = tt(pool, wl[:, :, cs], as2(r.t), f32(wh[:, :, cs]), ALU.subtract, sem("pool_kvl"))
                            r.free = [wkv]
                    for i in range(2):
                        for ct in (CTh[i], CTl[i]):
                            z = ct[:, :, S:SP]
                            wkv = pool.do(lambda e, z=z: e.memset(z.bitcast(F), 0.0), sem("pool_kvl"))
                    wkv_ready = [wkv]
            end_phase()

            with ExitStack() as s2:
                Kh = alloc(s2, f"Kh{half}", [128, NKV, SP], R)
                Kl = alloc(s2, f"Kl{half}", [128, NKV, SP], R)
                Vh = alloc(s2, f"Vh{half}", [128, 3, NKV * 128], R)
                Vl = alloc(s2, f"Vl{half}", [128, 3, NKV * 128], R)
                PT = Ring([Slot((alloc(s2, f"PTh{half}_{i}", [128, 3, 2 * T], R),
                                 alloc(s2, f"PTl{half}_{i}", [128, 3, 2 * T], R))) for i in range(2)])
                craw = Ring([Slot(alloc(s2, f"craw{half}_{i}", [128, 3, C]), sem(f"dma_craw{i}")) for i in range(2)])
                SC = Ring([Slot(alloc(s2, f"SC{half}_{i}", [T, 2, S])) for i in range(2)])
                PR = Ring([Slot(alloc(s2, f"PR{half}_{i}", [T, 2, S])) for i in range(2)])
                mx = Ring([Slot(alloc(s2, f"mx{half}_{i}", [T, 4, 2])) for i in range(3)])
                SB = Ring(banks[0:2])
                JB = Ring(banks[2:5])
                BA, BB, OB = banks[5], banks[6], banks[7]
                ct_ready, ct_free = {}, {}
                mb_ready, mb_free = {}, {}
                k_ready, k_free = {}, [None] * NKV
                v_ready, v_free = {}, [[], []]

                def prepare_ctx(bl):
                    b, i = b0 + bl, bl % 2
                    r = craw.next()
                    sp.wait(*r.free)
                    dma(sp, r.t[:, 0:2, :], ctx_in[b, 0:256, :].rearrange("(c p) d -> p c d", p=128), r.sem)
                    tok = dma(sp, r.t[0:S - 256, 2, :], ctx_in[b, 256:S, :], r.sem)
                    dve.wait(*mb_free.get(bl - 2, []))
                    mb_ready[bl] = ts(dve, mb[i][:, :], mask8[:, b * S:(b + 1) * S], 1.0, BIG,
                                      ALU.subtract, ALU.mult, sem("dve_mb"))
                    for k in range(2):
                        bk = JB.next()
                        pe.wait(tok, *bk.free)
                        for c, (o, n) in enumerate(CH):
                            t = turn(bk.t[:, o:o + n], r.t[0:n, c, k * 128:(k + 1) * 128], ident[0:n, 0:n],
                                     sem("pe_ct") if c == 2 else None)
                        ct_ready[bl] = split(bk.t[:, 0:S], CTh[i][:, k, 0:S], CTl[i][:, k, 0:S], "ct", t,
                                             ct_free.get(bl - 2, []))
                        bk.free = [ct_ready[bl]]
                    r.free = [t]

                def project_k(bl, g):
                    i, bk, gs = bl % 2, JB.next(), slice(g * 128, (g + 1) * 128)
                    pe.wait(ct_ready[bl], *bk.free, *wkv_ready)
                    for k in range(2):
                        t = mm3(bk.t[:, 0:SP], WKh[:, k, gs], WKl[:, k, gs], CTh[i][:, k, :], CTl[i][:, k, :],
                                k == 0, k == 1, sem("pe_k"))
                    k_ready[bl, g] = split(bk.t[:, 0:SP], Kh[:, g, :], Kl[:, g, :], "k", t,
                                           [k_free[g]] if k_free[g] else [])
                    bk.free = [k_ready[bl, g]]
                    ct_free[bl] = [t]

                def project_v(bl, hv, c):
                    i, bk = bl % 2, JB.next()
                    o, n = CH[c]
                    vs = slice(hv * 512, (hv + 1) * 512)
                    pe.wait(ct_ready[bl], *bk.free, *wkv_ready)
                    for k in range(2):
                        t = mm3(bk.t[0:n, :], CTh[i][:, k, o:o + n], CTl[i][:, k, o:o + n], WVh[:, k, vs], WVl[:, k, vs],
                                k == 0, k == 1, sem("pe_v"))
                    v_ready[bl, hv] = split(bk.t[0:n, :], Vh[0:n, c, vs], Vl[0:n, c, vs], "v", t, v_free[hv])
                    bk.free = [v_ready[bl, hv]]
                    ct_free[bl] = [t]

                def scores(bl, g):
                    qs = slice(bl * T, (bl + 1) * T)
                    sc, m = SC.next(), mx.next()
                    mi = bl % 2
                    toks = []
                    for h in range(2):
                        bk = SB.next()
                        pe.wait(k_ready[bl, g], *bk.free)
                        t = mm3(bk.t[0:T, 0:SP], QOh[:, 2 * g + h, qs], QOl[:, 2 * g + h, qs], Kh[:, g, :], Kl[:, g, :],
                                True, True, sem("pe_s"))
                        dve.wait(t, mb_ready[bl], *sc.free, *m.free)
                        o, a, bmask, acc = sc.t[:, h, :], bk.t[0:T, 0:S], mb[mi][:, :], m.t[:, 0, h:h + 1]
                        t2 = dve.do(lambda e, o=o, a=a, bm=bmask, acc=acc: e.tensor_tensor_reduce(
                            o, a, bm, 1.0, -3.0e38, ALU.add, ALU.max, acc), sem("dve_smax"))
                        bk.free = [t2]
                    k_free[g] = t
                    mb_free[bl] = [t2]
                    dve.wait(t2)
                    return sc, m, ts(dve, m.t[:, 1, :], m.t[:, 0, :], -XS, None, ALU.mult, s=sem("dve_nmx"))

                def exps(sc, m, t):
                    act.wait(t)
                    for h in range(2):
                        e_tok = activate(sc.t[:, h, :], sc.t[:, h, :], ACT.Exp, sem("act_exp"), bias=m.t[:, 1, h:h + 1],
                                         scale=XS, accum_out=m.t[:, 2, h:h + 1])
                    return e_tok

                def normalise(sc, m, t, bl):
                    dve.wait(t)
                    t = recip(m.t[:, 3, :], m.t[:, 2, :], sem("dve_rec"))
                    p = PR.next()
                    pool.wait(t, c_any, *p.free)
                    for h in range(2):
                        t = ts(pool, p.t[:, h, :], sc.t[:, h, :], m.t[:, 3, h:h + 1],
                               anyv[:, b0 + bl:b0 + bl + 1], ALU.mult, ALU.mult, sem("pool_p"))
                    sc.free = [t]
                    m.free = [t]
                    return p, t

                def turn_p(p, t):
                    pt = PT.next()
                    pe.wait(t, *BA.free, *BB.free)
                    for c, (o, n) in enumerate(CH):
                        for h in range(2):
                            dst = BA.t[:, (2 * c + h) * T:(2 * c + h + 1) * T] if c < 2 else BB.t[0:n, h * T:(h + 1) * T]
                            tk = turn(dst, p.t[:, h, o:o + n], ident[0:T, 0:T],
                                      sem("pe_pt") if h == 1 and c > 0 else None)
                            if c == 1 and h == 1:
                                t_a = tk
                    p.free = [tk]
                    ph, pl = pt.t
                    BA.free = [split(BA.t[:, 0:4 * T], ph[:, 0:2, :].rearrange("p a b -> p (a b)"),
                                     pl[:, 0:2, :].rearrange("p a b -> p (a b)"), "pt", t_a, pt.free)]
                    n = CH[2][1]
                    t2 = split(BB.t[0:n, 0:2 * T], ph[0:n, 2, :], pl[0:n, 2, :], "pt", tk)
                    BB.free = [t2]
                    return pt, t2

                def weighted(bl, g, pt, t):
                    ph, pl = pt.t
                    gs = slice(g * 128, (g + 1) * 128)
                    pe.wait(t, v_ready[bl, g // 4], *OB.free)
                    for c, (_, n) in enumerate(CH):
                        tk = mm3(OB.t[:, 0:2 * T], Vh[0:n, c, gs], Vl[0:n, c, gs], ph[0:n, c, :], pl[0:n, c, :],
                                 c == 0, c == 2, sem("pe_o"))
                    pt.free = [tk]
                    v_free[g // 4] = [tk]
                    qs = slice(bl * T, (bl + 1) * T)
                    src = OB.t[:, 0:2 * T].rearrange("p (h q) -> p h q", h=2)
                    o_tok = split(src, QOh[:, 2 * g:2 * g + 2, qs], QOl[:, 2 * g:2 * g + 2, qs], "o", tk)
                    OB.free = [o_tok]
                    return o_tok

                pe.wait(q_ready)
                prepare_ctx(0)
                prepare_ctx(1)
                for g in range(NKV):
                    project_k(0, g)
                for c in range(3):
                    project_v(0, 0, c)
                steps = [(bl, g) for bl in range(HB) for g in range(NKV)]
                soft, turned = {}, {}
                for i in range(len(steps) + 2):
                    bl, g = steps[i] if i < len(steps) else (HB, i - len(steps))
                    if bl < HB:
                        sc, m, t = scores(bl, g)
                        e_tok = exps(sc, m, t)
                        if bl + 1 < HB:
                            project_k(bl + 1, g)
                    if 1 <= i <= len(steps):
                        turned[i - 1] = turn_p(*soft.pop(i - 1))
                    if bl < HB:
                        soft[i] = normalise(sc, m, e_tok, bl)
                    if bl < HB and 2 <= g <= 4:
                        project_v(bl, 1, g - 2)
                    if i >= 2:
                        o_ready = weighted(*steps[i - 2], *turned.pop(i - 2))
                    if bl < HB:
                        if bl + 1 < HB and g >= 5:
                            project_v(bl + 1, 0, g - 5)
                        if g == NKV - 1 and bl + 2 < HB:
                            prepare_ctx(bl + 2)
            end_phase()

            with ExitStack() as s3:
                X = alloc(s3, f"Xb{half}", [T, HB, D])
                YT = alloc(s3, f"YT{half}", [128, KD, HT])
                wr = Ring([Slot(alloc(s3, f"wo{half}_{i}", [128, 2, 4, 128], R)) for i in range(6)])
                xt = dma(sp, X[:, :, :], xin[:, b0:b0 + HB, :], sem("dma_x"))
                Wov = Wo.rearrange("(n p) f -> p n f", p=128)
                srcs = [[(whole, Wov[:, 4 * u:4 * u + 4, f * 128:(f + 1) * 128])] for f in range(KD) for u in range(4)]
                pe.wait(o_ready)
                ys = []
                for n, (w, ready) in enumerate(weight_stream(wr, srcs, 4)):
                    f, u = n // 4, n % 4
                    bk = banks[f]
                    pe.wait(ready, *bk.free)
                    for k in range(4):
                        t = mm3(bk.t[:, 0:HT], w.t[:, 0, k, :], w.t[:, 1, k, :], QOh[:, 4 * u + k, :], QOl[:, 4 * u + k, :],
                                u == 0 and k == 0, k == 3 and u == 3, sem("pe_wo"), k == 3)
                    w.free = [t]
                    if u == 3:
                        act.wait(t)
                        ys.append(activate(YT[:, f, :], bk.t[:, 0:HT], ACT.Copy, sem("act_yt")))
                        bk.free = [ys[-1]]
                for i in range(HB):
                    bk = banks[4 + i]
                    pe.wait(ys[-1], *bk.free)
                    for f in range(KD):
                        t = turn(bk.t[0:T, f * 128:(f + 1) * 128], YT[:, f, i * T:(i + 1) * T], ident[:, :],
                                 sem("pe_turn") if f == KD - 1 else None)
                    dve.wait(t, xt, c_tanh)
                    t = stt(X[:, i, :], bk.t[0:T, :], tgx[:, 0:1], X[:, i, :], ALU.mult, ALU.add, sem("dve_x1"))
                    bk.free = [t]
                sp.wait(t)
                done_x1.append(dma(sp, x1[:, b0:b0 + HB, :], X[:, :, :], sem("dma_x1")))
            sp.wait(*done_x1)
            end_phase()

    with ExitStack() as s4:
        Z = alloc(s4, "Z", [T, B, D])
        CXh = alloc(s4, "CXh", [128, KD, TT], R)
        CXl = alloc(s4, "CXl", [128, KD, TT], R)
        causal = alloc(s4, "causal", [T, 4, T])
        causb = alloc(s4, "causb", [T, 4, T], BF)
        identb = alloc(s4, "identb", [T, T], BF)
        cosT = alloc(s4, "cosT", [128, 4, T])
        sinT = alloc(s4, "sinT", [128, 4, T])
        bqc = alloc(s4, "bqc", [128, KD])
        bkc = alloc(s4, "bkc", [128, KD])
        bvb = alloc(s4, "bvb", [T, D])
        QT = alloc(s4, "QT", [128, KD, TT])
        KT = alloc(s4, "KT", [128, KD, TT])
        V = alloc(s4, "V", [T, B, D])
        zt = dma(sp, Z[:, :, :], x1, sem("dma_z"))
        for i in range(4):
            dma(act, causal[:, i, :], c_causal, sem("dma_c2"))
            dma(act, cosT[:, i, :], c_cos, sem("dma_c2"))
            dma(act, sinT[:, i, :], c_sin, sem("dma_c2"))
        dma_columns(act, bqc[:, :], b_q.rearrange("(k p) -> p k", p=128), sem("dma_c2"))
        dma_columns(act, bkc[:, :], b_k.rearrange("(k p) -> p k", p=128), sem("dma_c2"))
        c2 = dma(act, bvb[:, :], bass.AP(b_v.tensor, 0, [[0, T], [1, D]]), sem("dma_c2"))
        pool.wait(c2)
        copy(pool, causb[:, :, :], causal[:, :, :], sem("pool_cb"))
        cb = copy(pool, identb[:, :], ident[0:T, 0:T], sem("pool_cb"))
        zrows = lambda i: Z[:, i, :]
        t = stats(zrows, 0, B, [zt])
        t = rstd(0, B, False, 1e-5, t)
        dve.wait(t)
        for i in range(B):
            t = ts(dve, Z[:, i, :], Z[:, i, :], mv[:, i, 0:1], rs[:, i:i + 1], ALU.subtract, ALU.mult, sem("dve_norm"))
        t = stats(zrows, 0, B, [t])
        h_ready = rstd(0, B, True, 1e-6, t)
        with ExitStack() as s5:
            H = alloc(s5, "H", [T, B, D])
            HTh = alloc(s5, "HTh", [128, KD, TT], R)
            HTl = alloc(s5, "HTl", [128, KD, TT], R)
            wr = Ring([Slot(alloc(s5, f"wf{i}", [128, 2, 4, 128], R)) for i in range(4)])
            PQ = Ring([Slot(alloc(s5, f"PQ{i}", [128, 3, HT])) for i in range(2)])
            dve.wait(h_ready)
            for i in range(B):
                t = ts(dve, H[:, i, :], Z[:, i, :], rs[:, i:i + 1], None, ALU.mult, s=sem("dve_norm"))
            for hf in range(2):
                ht = to_features(lambda i: H[:, i, :], hf * HB, HB, HTh, HTl, hf * HT, [t], "ht", ln1c)
            srcs = []
            for w_ in (wq, wk):
                v_ = w_.rearrange("(k p) n -> p k n", p=128)
                srcs += [[(whole, v_[:, :, m * 128:(m + 1) * 128])] for m in range(KD)]
            v_ = wv.rearrange("(k p) n -> p k n", p=128)
            srcs += [[(whole, v_[:, :, m * 128:(m + 1) * 128])] for m in range(KD)]
            qk_ready = None
            stream = weight_stream(wr, srcs, 3)
            for n in range(8):
                w, ready = next(stream)
                dst, bias = (QT, bqc) if n < 4 else (KT, bkc)
                m = n % 4
                for hf in range(2):
                    hs = slice(hf * HT, (hf + 1) * HT)
                    bk_ = banks[(2 * n + hf) % 8]
                    pe.wait(ready, ht, *bk_.free)
                    for k in range(KD):
                        t = mm3(bk_.t[:, 0:HT], w.t[:, 0, k, :], w.t[:, 1, k, :], HTh[:, k, hs], HTl[:, k, hs],
                                k == 0, k == KD - 1, sem("pe_f"))
                    p = PQ.next()
                    act.wait(t, c2, *p.free)
                    t2 = activate(p.t[:, 0, :], bk_.t[:, 0:HT], ACT.Identity, sem("act_f"), bias=bias[:, m:m + 1])
                    bk_.free = [t2]
                    dve.wait(t2)
                    o, a = p.t[:, 1, :], p.t[:, 0, :]
                    t3 = dve.do(lambda e, o=o, a=a: e.stream_shuffle(o, a, SWAP), sem("dve_shuf"))
                    pool.wait(t2, c2, *p.free)
                    q4 = lambda ap: ap.rearrange("p (b t) -> p b t", t=T)
                    t4 = tt(pool, q4(p.t[:, 2, :]), q4(p.t[:, 0, :]), cosT[:, :, :], ALU.mult, sem("pool_cos"))
                    dve.wait(t3)
                    t5 = tt(dve, q4(p.t[:, 1, :]), q4(p.t[:, 1, :]), sinT[:, :, :], ALU.mult, sem("dve_sin"))
                    dve.wait(t4, t5)
                    qk_ready = tt(dve, dst[:, m, hs], p.t[:, 1, :], p.t[:, 2, :], ALU.add, sem("dve_rope"))
                    p.free = [qk_ready]
                w.free = [t]
            vw = [next(stream) for _ in range(KD)]
            for b in range(B):
                bk_ = banks[b]
                bs = slice(b * T, (b + 1) * T)
                for m in range(KD):
                    pe.wait(vw[m][1], *bk_.free)
                    w = vw[m][0]
                    for k in range(KD):
                        t = mm3(bk_.t[0:T, m * 128:(m + 1) * 128], HTh[:, k, bs], HTl[:, k, bs], w.t[:, 0, k, :], w.t[:, 1, k, :],
                                k == 0, k == KD - 1, sem("pe_f"))
                dve.wait(t, c2)
                v_tok = tt(dve, V[:, b, :], bk_.t[0:T, :], bvb[:, :], ALU.add, sem("dve_v"))
                bk_.free = [v_tok]
        end_phase()

        with ExitStack() as s6:
            PF = Ring([Slot(alloc(s6, f"PF{i}", [T, 4, T])) for i in range(4)])
            PTf = Ring([Slot(alloc(s6, f"PTf{i}", [T, 4, T])) for i in range(3)])
            sm = Ring([Slot(alloc(s6, f"sm{i}", [T, 4, 4])) for i in range(4)])
            FB, TB, OB = Ring(banks[0:3]), Ring(banks[3:6]), Ring(banks[6:8])

            def f_scores(b, i):
                bs, ps = slice(b * T, (b + 1) * T), slice(32 * i, 32 * i + 32)
                p, m, bk_ = PF.next(), sm.next(), FB.next()
                pe.wait(qk_ready, cb, *bk_.free)
                matmul(bk_.t[0:T, 0:4 * T], identb[:, :], causb[:, :, :].rearrange("p a b -> p (a b)"), True, False)
                for c in range(4):
                    t = matmul(bk_.t[0:T, c * T:(c + 1) * T], QT[ps, c, bs], KT[ps, c, bs], False, c == 3,
                               sem("pe_fs") if c == 3 else None)
                dve.wait(t, *m.free)
                t = reduce(m.t[:, 0, :], bk_.t[0:T, 0:4 * T].rearrange("p (a b) -> p a b", a=4), ALU.max, sem("dve_fm"))
                dve.wait(t)
                t = ts(dve, m.t[:, 1, :], m.t[:, 0, :], -FS, None, ALU.mult, s=sem("dve_fn"))
                act.wait(t, *p.free)
                for c in range(4):
                    t = activate(p.t[:, c, :], bk_.t[0:T, c * T:(c + 1) * T], ACT.Exp,
                                 sem("act_fe") if c == 3 else None, bias=m.t[:, 1, c:c + 1], scale=FS,
                                 accum_out=m.t[:, 2, c:c + 1])
                bk_.free = [t]
                return p, m, t

            def f_norm(p, m, t):
                dve.wait(t)
                t = recip(m.t[:, 3, :], m.t[:, 2, :], sem("dve_fr"))
                dve.wait(t)
                r4 = m.t[:, 3, :].rearrange("p (a o) -> p a o", o=1).broadcast_to([T, 4, T])
                t = tt(dve, p.t[:, :, :], p.t[:, :, :], r4, ALU.mult, sem("dve_fp"))
                m.free = [t]
                return p, t

            def f_turn(i, p, t):
                pt, bk_ = PTf.next(), TB.next()
                pe.wait(t, *bk_.free)
                for c in range(4):
                    tk = turn(bk_.t[0:T, c * T:(c + 1) * T], p.t[:, c, :], ident[0:T, 0:T], sem("pe_ft") if c == 3 else None)
                p.free = [tk]
                dst = pt.t[:, :, :].rearrange("p a b -> p (a b)")
                if i % 2:
                    dve.wait(tk, *pt.free)
                    t = copy(dve, dst, bk_.t[0:T, 0:4 * T], sem("dve_ft"))
                else:
                    act.wait(tk, *pt.free)
                    t = activate(dst, bk_.t[0:T, 0:4 * T], ACT.Copy, sem("act_ft"))
                bk_.free = [t]
                return pt, t

            def f_out(b, i, pt, t):
                if i == 0:
                    OB.next()
                bk_ = OB.slots[(OB.n - 1) % 2]
                pe.wait(t, v_tok, *bk_.free)
                for c in range(4):
                    hcol = (4 * c + i) * FD
                    t = matmul(bk_.t[32 * i:32 * i + 32, c * T:(c + 1) * T], V[:, b, hcol:hcol + FD],
                               pt.t[:, c, :], True, True, sem("pe_fo") if c == 3 else None)
                pt.free = [t]
                if i == 3:
                    bs = slice(b * T, (b + 1) * T)
                    src = bk_.t[:, 0:4 * T].rearrange("p (a b) -> p a b", a=4)
                    t = split(src, CXh[:, :, bs], CXl[:, :, bs], "cx", t)
                    bk_.free = [t]
                return t

            units = [(b, i) for b in range(B) for i in range(4)]
            raised, normed, turned = {}, {}, {}
            for n in range(len(units) + 3):
                if n < len(units):
                    raised[n] = f_scores(*units[n])
                if 1 <= n <= len(units):
                    normed[n - 1] = f_norm(*raised.pop(n - 1))
                if 2 <= n <= len(units) + 1:
                    turned[n - 2] = f_turn(units[n - 2][1], *normed.pop(n - 2))
                if n >= 3:
                    cx_ready = f_out(*units[n - 3], *turned.pop(n - 3))
        end_phase()

        with ExitStack() as s7:
            YT = alloc(s7, "YTf", [128, KD, TT])
            wr = Ring([Slot(alloc(s7, f"wof{i}", [128, 2, 4, 128], R)) for i in range(3)])
            v_ = wo.rearrange("(k p) n -> p k n", p=128)
            srcs = [[(whole, v_[:, :, m * 128:(m + 1) * 128])] for m in range(KD)]
            ys = None
            for m, (w, ready) in enumerate(weight_stream(wr, srcs, 2)):
                for hf in range(2):
                    hs = slice(hf * HT, (hf + 1) * HT)
                    bk_ = banks[2 * m + hf]
                    pe.wait(ready, cx_ready, *bk_.free)
                    for k in range(KD):
                        t = mm3(bk_.t[:, 0:HT], w.t[:, 0, k, :], w.t[:, 1, k, :], CXh[:, k, hs], CXl[:, k, hs],
                                k == 0, k == KD - 1, sem("pe_f"))
                    act.wait(t)
                    ys = activate(YT[:, m, hs], bk_.t[:, 0:HT], ACT.Copy, sem("act_yt"))
                    bk_.free = [ys]
                w.free = [t]
            for b in range(B):
                bk_ = banks[b]
                pe.wait(ys, *bk_.free)
                for f in range(KD):
                    t = turn(bk_.t[0:T, f * 128:(f + 1) * 128], YT[:, f, b * T:(b + 1) * T], ident[:, :],
                             sem("pe_turn") if f == KD - 1 else None)
                dve.wait(t)
                x2_tok = tt(dve, Z[:, b, :], bk_.t[0:T, :], Z[:, b, :], ALU.add, sem("dve_x2"))
                bk_.free = [x2_tok]
            sp.wait(x2_tok)
            done_x2 = dma(sp, s_x2.rearrange("b t d -> t b d"), Z[:, :, :], sem("dma_x2"))
            sp.wait(done_x2)
            t = stats(zrows, 0, B, [x2_tok])
            t = rstd(0, B, True, 1e-6, t)
        end_phase()

    keep = ExitStack()
    Y = alloc(keep, "Y", [128, KD, TT])
    with ExitStack() as s8:
        H2h = alloc(s8, "H2h", [128, KD, TT], R)
        H2l = alloc(s8, "H2l", [128, KD, TT], R)
        with ExitStack() as s9:
            H = alloc(s9, "H2", [T, B, D])
            WR = alloc(s9, "WR", [128, KD, 10])
            WRh = alloc(s9, "WRh", [128, KD, 10], R)
            WRl = alloc(s9, "WRl", [128, KD, 10], R)
            L = alloc(s9, "L", [T, B, 10])
            pr = alloc(s9, "pr", [T, B, NE])
            w8 = alloc(s9, "w8", [T, B, NE])
            s1_ = alloc(s9, "s1_", [T, B, NE])
            s2_ = alloc(s9, "s2_", [T, B, NE])
            io8 = alloc(s9, "io8", [T, B, NE])
            r1 = alloc(s9, "r1", [T, 4, B])
            comb = alloc(s9, "comb", [T, B, NE + 1])
            combT = alloc(s9, "combT", [NE + 1, TT])
            ht = dma(sp, H[:, :, :], s_x2.rearrange("b t d -> t b d"), sem("dma_z"))
            z_tok = pool.do(lambda e: e.memset(WR[:, :, :], 0.0), sem("pool_wr"))
            for i in range(NE):
                zi = io8[:, :, i:i + 1]
                io_tok = pool.do(lambda e, zi=zi, i=i: e.memset(zi, float(NE - i)), sem("pool_wr"))
            sp.wait(z_tok)
            dma(sp, WR[:, :, 0:NE], w_router.rearrange("(k p) n -> p k n", p=128), sem("dma_wr"))
            wt = dma_columns(sp, WR[:, :, NE:NE + 1], sh_eg.rearrange("(k p) n -> p k n", p=128), sem("dma_wr"))
            pool.wait(wt)
            h = copy(pool, WRh[:, :, :], WR[:, :, :], sem("pool_wr"))
            pool.wait(h)
            wr_ready = tt(pool, WRl[:, :, :], WR[:, :, :], f32(WRh[:, :, :]), ALU.subtract, sem("pool_wr"))
            dve.wait(ht)
            for i in range(B):
                t = ts(dve, H[:, i, :], H[:, i, :], rs[:, i:i + 1], None, ALU.mult, s=sem("dve_norm"))
            for hf in range(2):
                h2 = to_features(lambda i: H[:, i, :], hf * HB, HB, H2h, H2l, hf * HT, [t], "ht", ln2c)
            bk_ = banks[4]
            pe.wait(h2, wr_ready, *bk_.free)
            for b in range(B):
                bs = slice(b * T, (b + 1) * T)
                for k in range(KD):
                    t = mm3(bk_.t[0:T, b * 10:b * 10 + 10], H2h[:, k, bs], H2l[:, k, bs], WRh[:, k, :], WRl[:, k, :],
                            k == 0, k == KD - 1, sem("pe_r"))
            dve.wait(t)
            sd = sem("dve_r")

            def link(t):
                dve.wait(t)

            t = copy(dve, L[:, :, :], bk_.t[0:T, 0:B * 10].rearrange("p (b n) -> p b n", n=10), sd)
            bk_.free = [t]
            l_tok = t
            link(t)
            wide = lambda i: r1[:, i, :].rearrange("p (b o) -> p b o", o=1).broadcast_to([T, B, NE])
            link(reduce(r1[:, 0, :], L[:, :, 0:NE], ALU.max, sd))
            t = tt(dve, pr[:, :, :], L[:, :, 0:NE], wide(0), ALU.subtract, sd)
            act.wait(t)
            t = activate(pr[:, :, :], pr[:, :, :], ACT.Exp, sem("act_r"))
            sg = activate(comb[:, :, NE:NE + 1], L[:, :, NE:NE + 1], ACT.Sigmoid, sem("act_r"))
            link(t)
            link(reduce(r1[:, 0, :], pr[:, :, :], ALU.add, sd))
            link(recip(r1[:, 1, :], r1[:, 0, :], sd))
            link(tt(dve, pr[:, :, :], pr[:, :, :], wide(1), ALU.mult, sd))
            dve.wait(io_tok)
            src, sels = pr, (s1_, s2_)
            for r in range(2):
                sl = sels[r]
                link(reduce(r1[:, 2, :], src[:, :, :], ALU.max, sd))
                link(tt(dve, sl[:, :, :], src[:, :, :], wide(2), ALU.is_equal, sd))
                link(tt(dve, sl[:, :, :], sl[:, :, :], io8[:, :, :], ALU.mult, sd))
                link(reduce(r1[:, 3, :], sl[:, :, :], ALU.max, sd))
                link(tt(dve, sl[:, :, :], io8[:, :, :], wide(3), ALU.is_equal, sd))
                if r == 0:
                    link(stt(w8[:, :, :], sl[:, :, :], -4.0, pr[:, :, :], ALU.mult, ALU.add, sd))
                    src = w8
            link(tt(dve, s1_[:, :, :], s1_[:, :, :], s2_[:, :, :], ALU.add, sd))
            t = tt(dve, comb[:, :, 0:NE], pr[:, :, :], s1_[:, :, :], ALU.mult, sd)
            for hf in range(2):
                bk_ = banks[5 + hf]
                pe.wait(t, sg, *bk_.free)
                for i in range(HB):
                    tk = turn(bk_.t[0:NE + 1, i * T:(i + 1) * T], comb[:, hf * HB + i, :], ident[0:T, 0:T],
                              sem("pe_turn") if i == HB - 1 else None)
                dve.wait(tk)
                ct = copy(dve, combT[:, hf * HT:(hf + 1) * HT], bk_.t[0:NE + 1, 0:HT], sem("dve_ct2"))
                bk_.free = [ct]
            sp.wait(ct)
            done_comb = dma(sp, s_comb, combT[:, :], sem("dma_comb"))
            sp.wait(done_comb)
        end_phase()

        HDh = alloc(s8, "HDh", [128, NJ, TT], R)
        HDl = alloc(s8, "HDl", [128, NJ, TT], R)
        wr = Ring([Slot(alloc(s8, f"wm{i}", [128, 2, 4, 128], R)) for i in range(4)])
        wd = Ring([Slot(alloc(s8, f"wd{i}", [128, 2, NJ, 128], R)) for i in range(2)])
        rd = Ring([Slot(alloc(s8, f"rd{i}", [128, NJ, 128]), sem(f"dma_rd{i}")) for i in range(2)])
        G = Ring([Slot(alloc(s8, f"G{i}", [128, TT]), sem(f"dma_g{i}")) for i in range(2)])
        TM = Ring([Slot(alloc(s8, f"TM{i}", [128, 2, HT])) for i in range(2)])
        GB, UB, YB = Ring(banks[0:2]), Ring(banks[2:4]), Ring(banks[4:8])
        dflat = w_down.rearrange("e i h -> (e i) h")
        srcs = []
        plans = []
        for grp in range(3):
            for j in range(NJ):
                if grp == 0:
                    js = slice(j * 128, (j + 1) * 128)
                    for w_ in (sh_gate, sh_up):
                        srcs.append([(whole, w_.rearrange("(k p) n -> p k n", p=128)[:, :, js])])
                    plans.append([(0, 128, NE)])
                    continue
                lo, segs = (grp - 1) * 4 * EI + j * 128, []
                hi = lo + 128
                at = lo
                while at < hi:
                    e = at // EI
                    end = min(hi, (e + 1) * EI)
                    segs.append((at - lo, end - at, e, at - e * EI))
                    at = end
                for w_ in (w_gate, w_up):
                    srcs.append([((lambda t, o=o, n=n: t[:, :, o:o + n]),
                                  w_[e].rearrange("(k p) n -> p k n", p=128)[:, :, a:a + n]) for o, n, e, a in segs])
                plans.append([(o, n, e) for o, n, e, _ in segs])
        stream = weight_stream(wr, srcs, 2)
        hd_free = []
        y_ready = None

        def load_down(grp, f):
            fs = slice(f * 128, (f + 1) * 128)
            base = sh_down if grp == 0 else dflat[(grp - 1) * 4 * EI:grp * 4 * EI, :]
            r = rd.next()
            sp.wait(*r.free)
            tok = dma(sp, r.t[:, :, :], base.rearrange("(j p) f -> p j f", p=128)[:, :, fs], r.sem)
            w = wd.next()
            act.wait(tok, *w.free)
            h = activate(w.t[:, 0, :, :], r.t[:, :, :], ACT.Copy, sem("act_wd"))
            pool.wait(h)
            ready = tt(pool, w.t[:, 1, :, :], r.t[:, :, :], f32(w.t[:, 0, :, :]), ALU.subtract, sem("pool_dl"))
            r.free = [ready]
            return w, ready

        for grp in range(3):
            downs, hd_ready = [], []
            for j in range(NJ):
                gt = G.next()
                sp.wait(*gt.free, done_comb)
                for o, n, e in plans[grp * NJ + j]:
                    g_tok = dma(sp, gt.t[o:o + n, :], bass.AP(s_comb.tensor, e * TT, [[0, n], [1, TT]]), gt.sem)
                wg, g_r = next(stream)
                wu, u_r = next(stream)
                for hf in range(2):
                    hs = slice(hf * HT, (hf + 1) * HT)
                    gb, ub = GB.next(), UB.next()
                    for w, ready, bk_ in ((wg, g_r, gb), (wu, u_r, ub)):
                        pe.wait(ready, h2, *bk_.free)
                        for k in range(KD):
                            t = mm3(bk_.t[:, 0:HT], w.t[:, 0, k, :], w.t[:, 1, k, :], H2h[:, k, hs], H2l[:, k, hs],
                                    k == 0, k == KD - 1, sem("pe_gu"))
                        if bk_ is gb:
                            t_g = t
                    tm = TM.next()
                    act.wait(t_g, *tm.free)
                    s_tok = activate(tm.t[:, 0, :], gb.t[:, 0:HT], ACT.Silu, sem("act_silu"))
                    gb.free = [s_tok]
                    dve.wait(s_tok, t)
                    m_tok = tt(dve, tm.t[:, 0, :], ub.t[:, 0:HT], tm.t[:, 0, :], ALU.mult, sem("dve_gu"))
                    ub.free = [m_tok]
                    pool.wait(m_tok, g_tok)
                    p_tok = tt(pool, tm.t[:, 1, :], tm.t[:, 0, :], gt.t[:, hs], ALU.mult, sem("pool_gu"))
                    act.wait(p_tok, *hd_free)
                    h_tok = activate(HDh[:, j, hs], tm.t[:, 1, :], ACT.Copy, sem("act_hd"))
                    dve.wait(h_tok)
                    hd_tok = tt(dve, HDl[:, j, hs], tm.t[:, 1, :], f32(HDh[:, j, hs]), ALU.subtract, sem("dve_hd"))
                    tm.free = [hd_tok]
                hd_ready.append([h_tok, hd_tok])
                wg.free = wu.free = [t]
                gt.free = [p_tok]
                if j in (NJ - 5, NJ - 3):
                    downs.append(load_down(grp, len(downs)))
            for f in range(KD):
                w, ready = downs[f]
                for hf in range(2):
                    hs = slice(hf * HT, (hf + 1) * HT)
                    bk_ = YB.next()
                    pe.wait(ready, *bk_.free)
                    for j in range(NJ):
                        pe.wait(*hd_ready[j])
                        t = mm3(bk_.t[:, 0:HT], w.t[:, 0, j, :], w.t[:, 1, j, :], HDh[:, j, hs], HDl[:, j, hs],
                                j == 0, j == NJ - 1, sem("pe_d"))
                    dve.wait(t)
                    if grp == 0:
                        y_ready = copy(dve, Y[:, f, hs], bk_.t[:, 0:HT], sem("dve_y"))
                    else:
                        dve.wait(y_ready)
                        y_ready = tt(dve, Y[:, f, hs], bk_.t[:, 0:HT], Y[:, f, hs], ALU.add, sem("dve_y"))
                    bk_.free = [y_ready]
                w.free = [t]
                hd_free = [t]
                if f + 2 < KD:
                    downs.append(load_down(grp, f + 2))
        end_phase()

    with ExitStack() as s10:
        X1 = Ring([Slot(alloc(s10, f"X1_{i}", [T, D]), sem(f"dma_e{i}")) for i in range(4)])
        X2 = Ring([Slot(alloc(s10, f"X2_{i}", [T, D])) for i in range(4)])
        for b in range(B):
            u, v = X1.next(), X2.next()
            sp.wait(*u.free)
            dma(sp, u.t[:, :], s_x1[b], u.sem)
            xt = dma(sp, v.t[:, :], s_x2[b], u.sem)
            bk_ = banks[b]
            pe.wait(y_ready, *bk_.free)
            for f in range(KD):
                t = turn(bk_.t[0:T, f * 128:(f + 1) * 128], Y[:, f, b * T:(b + 1) * T], ident[:, :],
                         sem("pe_turn") if f == KD - 1 else None)
            dve.wait(t, xt)
            t = tt(dve, v.t[:, :], bk_.t[0:T, :], v.t[:, :], ALU.add, sem("dve_e1"))
            bk_.free = [t]
            dve.wait(t)
            t = stt(v.t[:, :], v.t[:, :], tgf[:, 0:1], u.t[:, :], ALU.mult, ALU.add, sem("dve_e2"))
            act.wait(t)
            u.free = [dma(act, out[b], v.t[:, :], sem(f"dma_out{b % 4}"))]
    keep.close()
    act.wait(*[tok for u in X1.slots for tok in u.free])
    sp.wait(done_x2, done_comb, *done_x1)

    with top:
        block = top.enter_context(nc.Block())

        @block.sync
        def _(eng):
            sp.play(eng)

        @block.scalar
        def _(eng):
            act.play(eng)

        @block.vector
        def _(eng):
            dve.play(eng)

        @block.gpsimd
        def _(eng):
            pool.play(eng)

        @block.tensor
        def _(eng):
            pe.play(eng)


_INS = ['x', 'ctx_1024', 'mask_BxS2_bf1', 'g_xattn', 'g_ffn', 'L0_xattn_Wq', 'L0_xattn_Wk', 'L0_xattn_Wv',
        'L0_xattn_Wo', 'L0_ffn_w_ln1', 'L0_ffn_wq', 'L0_ffn_bq', 'L0_ffn_wk', 'L0_ffn_bk', 'L0_ffn_wv',
        'L0_ffn_bv', 'L0_ffn_wo', 'L0_ffn_w_ln2', 'L0_ffn_w_router', 'L0_ffn_w_gate_e', 'L0_ffn_w_up_e',
        'L0_ffn_w_down_e', 'L0_ffn_w_sh_gate', 'L0_ffn_w_sh_up', 'L0_ffn_w_sh_down', 'L0_ffn_w_sh_eg']


def _constants():
    ident = np.eye(128, dtype=np.float32)
    causal = np.where(np.tril(np.ones((T, T), bool)), np.float32(0), np.float32(-BIG)).astype(np.float32)
    inv = (np.float32(1.0) / np.power(np.float32(1.0e6), np.arange(0, FD, 2, dtype=np.float32) / np.float32(FD))).astype(np.float32)
    ang = (np.arange(T, dtype=np.float32)[:, None] * inv[None, :]).astype(np.float32)
    emb = np.concatenate([ang, ang], axis=-1)
    cos = np.cos(emb).astype(np.float32).T
    sin = np.sin(emb).astype(np.float32).T
    sin = np.concatenate([-sin[:FD // 2], sin[FD // 2:]], axis=0)
    return {'c_id': ident, 'c_causal': causal, 'c_cos': np.ascontiguousarray(np.tile(cos, (4, 1))),
            'c_sin': np.ascontiguousarray(np.tile(sin, (4, 1)))}


def kernel(**inputs):
    import numpy as _np
    import concourse.bacc as _bacc
    from concourse import mybir as _mybir
    from concourse.bass_utils import run_bass_kernel_spmd as _run

    nc = _bacc.Bacc("TRN2", target_bir_lowering=False, num_devices=1)
    arrays, args = {}, []
    for name in _INS:
        a = _np.ascontiguousarray(inputs[name])
        if a.dtype == _np.bool_:
            a = a.view(_np.uint8)
        arrays[f"in_{name}_dram"] = a
        args.append(nc.dram_tensor(f"in_{name}_dram", a.shape, _mybir.dt.from_np(a.dtype), kind="ExternalInput").ap())
    for name, a in _constants().items():
        arrays[f"in_{name}_dram"] = a
        args.append(nc.dram_tensor(f"in_{name}_dram", a.shape, _mybir.dt.from_np(a.dtype), kind="ExternalInput").ap())
    for name, shape in (("s_x1", (B, T, D)), ("s_x2", (B, T, D)), ("s_comb", (NE + 1, TT))):
        args.append(nc.dram_tensor(name, shape, F, kind="Internal").ap())
    args.append(nc.dram_tensor("out_0_dram", (B, T, D), F, kind="ExternalOutput").ap())
    flamingo_kernel(nc, *args)
    r = _run(nc, [arrays], core_ids=[0])
    return r.results[0]["out_0_dram"]
```

```python
from contextlib import ExitStack

import numpy as np
import concourse.bass as bass
from concourse import mybir

F = mybir.dt.float32
R = mybir.dt.float32r
BF = mybir.dt.bfloat16
U8 = mybir.dt.uint8
ALU = mybir.AluOpType
ACT = mybir.ActivationFunctionType
AX = mybir.AxisListType.X

B, T, D = 8, 100, 512
S, C = 361, 256
SP = 362
NH, NKV, HD = 16, 8, 128
FH, FD = 16, 32
NE, EI = 8, 352
HB = 4
HT = HB * T
TT = B * T
KD = D // 128
CH = [(0, 128), (128, 128), (256, S - 256)]
NJ = 11
BIG = 1.0e30
SB_START = 16512
SB_END = 229344
XS = float(1.0 / np.sqrt(np.float32(HD)))
FS = float(FD) ** -0.5
SWAP = [(i + 16) % 32 for i in range(32)]


class Sem:

    def __init__(self, handle):
        self.handle = handle
        self.count = 0

    def after(self, step):
        self.count += step
        return (self, self.count)


class Queue:

    def __init__(self):
        self.items = []
        self.seen = {}

    def wait(self, *tokens):
        for sem, value in tokens:
            if self.seen.get(sem, 0) < value:
                self.seen[sem] = value
                self.items.append((sem.handle, value, None))

    def do(self, emit, sem=None, step=1):
        self.items.append((sem.handle if sem else None, step, emit))
        return sem.after(step) if sem else None

    def play(self, eng):
        for handle, n, emit in self.items:
            if emit is None:
                eng.wait_ge(handle, n)
            elif handle is None:
                emit(eng)
            else:
                emit(eng).then_inc(handle, n)


class Region:

    def __init__(self, nc, start, end=SB_END):
        self.nc, self.at, self.end = nc, start, end

    def place(self, name, shape, dt=F):
        n = int(np.prod(shape[1:])) * {F: 4, R: 4, BF: 2, U8: 1}[dt]
        t = self.nc.alloc_sbuf_tensor_at(name, shape, dt, offset=self.at)
        self.at += (n + 31) // 32 * 32
        assert self.at <= self.end, (name, self.at, self.end)
        return t


class Slot:

    def __init__(self, t, sem=None):
        self.t = t
        self.sem = sem
        self.free = []


class Ring:
    def __init__(self, slots):
        self.slots = slots
        self.n = 0

    def next(self):
        self.n += 1
        return self.slots[(self.n - 1) % len(self.slots)]


def f32(ap):
    return ap.bitcast(F)


def flamingo_kernel(nc, x, ctx_in, mask, g_x, g_f, Wq, Wk, Wv, Wo, w_ln1, wq, b_q, wk, b_k, wv, b_v, wo,
                    w_ln2, w_router, w_gate, w_up, w_down, sh_gate, sh_up, sh_down, sh_eg,
                    c_id, c_causal, c_cos, c_sin, s_x1, s_x2, s_comb, out):
    top = ExitStack()
    pe, act, dve, pool, sp = Queue(), Queue(), Queue(), Queue(), Queue()
    names = {}

    def sem(name):
        if name not in names:
            names[name] = Sem(top.enter_context(nc.semaphore(name)))
        return names[name]

    def matmul(o, a, b, start, stop, s=None):
        return pe.do(lambda e: e.matmul(o, a, b, start=start, stop=stop, skip_group_check=True), s)

    def mm3(o, ah, al, bh, bl, first, last, s=None, mark=None):
        matmul(o, ah, bh, first, False)
        matmul(o, ah, bl, False, False)
        return matmul(o, al, bh, False, last, s if (last if mark is None else mark) else None)

    def turn(o, i, ident, s=None):
        return pe.do(lambda e: e.transpose(o, i, ident), s)

    def activate(o, i, func, s=None, **kw):
        return act.do(lambda e: e.activation(o, i, func, **kw), s)

    def tt(q, o, a, b, op, s=None):
        return q.do(lambda e: e.tensor_tensor(o, a, b, op), s)

    def ts(q, o, a, s1, s2, op0, op1=None, s=None):
        if op1 is None:
            return q.do(lambda e: e.tensor_scalar(o, a, s1, None, op0), s)
        return q.do(lambda e: e.tensor_scalar(o, a, s1, s2, op0, op1), s)

    def stt(o, a, sc, b, op0, op1, s=None):
        return dve.do(lambda e: e.scalar_tensor_tensor(out=o, in0=a, scalar=sc, in1=b, op0=op0, op1=op1), s)

    def copy(q, o, i, s=None):
        return q.do(lambda e: e.tensor_copy(o, i), s)

    def reduce(o, i, op, s=None):
        return dve.do(lambda e: e.tensor_reduce(o, i, AX, op), s)

    def recip(o, i, s=None):
        return dve.do(lambda e: e.reciprocal(o, i), s)

    def dma(q, o, i, s):
        return q.do(lambda e: e.dma_start(o, i), s, 16)

    def dma_columns(q, o, i, s):
        return q.do(lambda e: e.dma_start(o, i, allow_slow_non_contiguous=True), s, 16)

    def split(src, hi, lo, name, ready, free=(), scale=None):
        act.wait(ready, *free)
        if scale is None:
            h = activate(hi, src, ACT.Copy, sem("act_" + name))
            dve.wait(h)
            return tt(dve, lo, src, f32(hi), ALU.subtract, sem("dve_" + name))
        h = activate(hi, src, ACT.Copy, sem("act_" + name), scale=scale)
        dve.wait(h)
        return stt(lo, src, scale, f32(hi), ALU.mult, ALU.subtract, sem("dve_" + name))

    banks = [Slot(top.enter_context(nc.psum_tensor(f"bank{i}", [128, 512], F))) for i in range(8)]

    P_ = Region(nc, SB_START)
    ident = P_.place("ident", [128, 128])
    mask8 = P_.place("mask8", [T, B * S], U8)
    anyv = P_.place("anyv", [T, B])
    gx = P_.place("gx", [T, 1])
    gf = P_.place("gf", [T, 1])
    tgx = P_.place("tgx", [T, 1])
    tgf = P_.place("tgf", [T, 1])
    stat = P_.place("stat", [T, B, 6])
    mv = P_.place("mv", [T, B, 2])
    rs = P_.place("rs", [T, B])
    ms = P_.place("ms", [T, B])
    eps1 = P_.place("eps1", [T, 1])
    eps2 = P_.place("eps2", [T, 1])
    raw = Ring([Slot(P_.place(f"raw{i}", [128, 4, 128]), sem(f"dma_raw{i}")) for i in range(4)])
    Z = P_.place("Z", [T, B, D])
    ffn0 = P_.at

    WKh = P_.place("WKh", [128, 2, NKV * 128], R)
    WKl = P_.place("WKl", [128, 2, NKV * 128], R)
    WVh = P_.place("WVh", [128, 2, NKV * 128], R)
    WVl = P_.place("WVl", [128, 2, NKV * 128], R)
    QOh = P_.place("QOh", [128, NH, HT], R)
    QOl = P_.place("QOl", [128, NH, HT], R)
    CTh = [P_.place(f"CTh{i}", [128, 2, SP], R) for i in range(2)]
    CTl = [P_.place(f"CTl{i}", [128, 2, SP], R) for i in range(2)]
    mb = P_.place("mb", [T, S])
    craw = Slot(P_.place("craw", [128, 3, C]), sem("dma_craw"))
    xring = Ring([Slot(P_.place(f"wx{i}", [128, 2, 4, 128], R)) for i in range(4)])
    work0 = P_.at

    A_ = Region(nc, work0)
    Kh = A_.place("Kh", [128, NKV, SP], R)
    Kl = A_.place("Kl", [128, NKV, SP], R)
    Vh = A_.place("Vh", [128, 3, NKV * 128], R)
    Vl = A_.place("Vl", [128, 3, NKV * 128], R)
    PT = Ring([Slot((A_.place(f"PTh{i}", [128, 3, 2 * T], R), A_.place(f"PTl{i}", [128, 3, 2 * T], R)))
               for i in range(2)])
    SC = Ring([Slot(A_.place(f"SC{i}", [T, 2, S])) for i in range(3)])
    mx = Ring([Slot(A_.place(f"mx{i}", [T, 4, 2])) for i in range(3)])

    C_ = Region(nc, work0)
    YT = C_.place("YT", [128, KD, HT])
    XR = C_.place("XR", [T, HB, D])
    X = C_.place("X", [T, HB, D])
    XTh = C_.place("XTh", [128, KD, HT], R)
    XTl = C_.place("XTl", [128, KD, HT], R)

    F_ = Region(nc, ffn0, work0)
    HTh = [F_.place(f"HTh{h}", [128, KD, HT], R) for h in range(2)]
    HTl = [F_.place(f"HTl{h}", [128, KD, HT], R) for h in range(2)]
    mid0 = F_.at
    QT, KT, V, CXh, CXl = ([None, None] for _ in range(5))

    def place_half(h):
        QT[h] = F_.place(f"QT{h}", [128, KD, HT])
        KT[h] = F_.place(f"KT{h}", [128, KD, HT])
        V[h] = F_.place(f"V{h}", [T, HB, D])
        CXh[h] = F_.place(f"CXh{h}", [128, KD, HT], R)
        CXl[h] = F_.place(f"CXl{h}", [128, KD, HT], R)

    place_half(0)
    PQ = Ring([Slot(F_.place(f"PQ{i}", [128, 3, HT])) for i in range(2)])
    half1 = F_.at
    place_half(1)
    bvb = F_.place("bvb", [T, D])
    after1 = F_.at
    ln2b = F_.place("ln2b", [T, D])
    causb = F_.place("causb", [T, 4, T], BF)
    identb = F_.place("identb", [T, T], BF)
    sm = Ring([Slot(F_.place(f"sm{i}", [T, 4, 4])) for i in range(4)])
    WR = F_.place("WR", [128, KD, 10])
    WRh = F_.place("WRh", [128, KD, 10], R)
    WRl = F_.place("WRl", [128, KD, 10], R)
    L = F_.place("L", [T, HB, 10])
    pr = F_.place("pr", [T, HB, NE])
    w8 = F_.place("w8", [T, HB, NE])
    sel1 = F_.place("sel1", [T, HB, NE])
    sel2 = F_.place("sel2", [T, HB, NE])
    io8 = F_.place("io8", [T, HB, NE])
    r1 = F_.place("r1", [T, 4, HB])
    comb = F_.place("comb", [T, HB, NE + 1])
    combT = F_.place("combT", [NE + 1, HT])

    E_ = Region(nc, work0 + 4 * (KD * HT + HB * D))
    cosT = E_.place("cosT", [128, 4, T])
    sinT = E_.place("sinT", [128, 4, T])
    bqc = E_.place("bqc", [128, KD])
    bkc = E_.place("bkc", [128, KD])
    ln1b = E_.place("ln1b", [T, D])
    causal = E_.place("causal", [T, T])
    HR = Ring([Slot(E_.place(f"HR{i}", [T, D])) for i in range(2)])
    fring = Ring([Slot(E_.place(f"wf{i}", [128, 2, 4, 128], R)) for i in range(6)])
    y1 = E_.at
    PF = Ring([Slot(E_.place(f"PF{i}", [T, 4, T])) for i in range(4)])
    PTf = Ring([Slot(E_.place(f"PTf{i}", [T, 4, T])) for i in range(3)])
    G = Ring([Slot(E_.place(f"G{i}", [128, HT]), sem(f"dma_g{i}")) for i in range(3)])
    YTf = Region(nc, work0).place("YTf", [128, KD, HT])

    H2 = Region(nc, ffn0, mid0)
    H2h = [H2.place(f"H2h{h}", [128, KD, HT], R) for h in range(2)]
    H2l = [H2.place(f"H2l{h}", [128, KD, HT], R) for h in range(2)]
    D0 = Region(nc, mid0, half1)
    D1 = Region(nc, half1, after1)
    HDh = [D0.place("HDh0", [128, NJ, HT], R), D1.place("HDh1", [128, NJ, HT], R)]
    HDl = [D0.place("HDl0", [128, NJ, HT], R), D1.place("HDl1", [128, NJ, HT], R)]
    TM = Ring([Slot(D0.place(f"TM{i}", [128, 2, HT])) for i in range(2)])
    Y_ = Region(nc, work0 + 4 * KD * HT, work0 + 4 * (KD * HT + HB * D))
    Y = [Y_.place("Y0", [128, KD, HT]), Region(nc, y1).place("Y1", [128, KD, HT])]
    OUT = Ring([Slot(o, sem(f"dma_out{i}")) for i, o in
                enumerate([Region(nc, ffn0 + i * 4 * D).place(f"OUT{i}", [T, D]) for i in range(4)])])
    x_ready = {}

    def load_x(half):
        for i in range(HB):
            b = half * HB + i
            x_ready[b] = dma(act, X[:, i, :], x[b], sem(f"dma_x{i}"))

    load_x(0)
    c_ident = dma(act, ident[:, :], c_id, sem("dma_ident"))
    c_mask = dma(act, mask8[:, :], bass.AP(mask.tensor, 0, [[0, T], [1, B * S]]), sem("dma_mask"))
    dma(act, gx[:, :], bass.AP(g_x.tensor, 0, [[0, T], [1, 1]]), sem("dma_small"))
    c_small = dma(act, gf[:, :], bass.AP(g_f.tensor, 0, [[0, T], [1, 1]]), sem("dma_small"))
    pool.do(lambda e: e.memset(eps1[:, :], 1e-5), sem("pool_eps"))
    c_eps = pool.do(lambda e: e.memset(eps2[:, :], 1e-6), sem("pool_eps"))
    act.wait(c_small)
    activate(tgx[:, :], gx[:, :], ACT.Tanh, sem("act_tanh"))
    c_tanh = activate(tgf[:, :], gf[:, :], ACT.Tanh, sem("act_tanh"))

    def whole(t):
        return t[:, :, :]

    def part(o, n):
        return lambda t: t[:, :, o:o + n]

    def rows4(t):
        return t[:, :, :].rearrange("p a b -> p (a b)").rearrange("p (k n) -> p k n", k=2)

    def kpn(w):
        return w.rearrange("(k p) n -> p k n", p=128)

    def load_unit(pieces):
        r = raw.next()
        sp.wait(*r.free)
        for view, src in pieces:
            tok = dma(sp, view(r.t), src, r.sem)
        return r, tok

    class Stream:

        def __init__(self, ring, sources, ahead):
            self.ring, self.sources, self.ahead, self.ready = ring, list(sources), ahead, []

        def fetch(self):
            if not self.sources:
                return
            r, tok = load_unit(self.sources.pop(0))
            w = self.ring.next()
            act.wait(tok, *w.free)
            h = activate(w.t[:, 0, :, :], r.t[:, :, :], ACT.Copy, sem("act_w"))
            pool.wait(h)
            lo = tt(pool, w.t[:, 1, :, :], r.t[:, :, :], f32(w.t[:, 0, :, :]), ALU.subtract, sem("pool_w"))
            r.free = [lo]
            self.ready.append((w, lo))

        def fill(self):
            while self.sources and len(self.ready) < self.ahead:
                self.fetch()

        def next(self):
            self.fetch()
            return self.ready.pop(0)

    def stats(row, i, ready):
        dve.wait(*ready)
        t = dve.do(lambda e: e.bn_stats(stat[:, i, :], row), sem("dve_bn"))
        dve.wait(t)
        return dve.do(lambda e: e.bn_aggr(mv[:, i, :], stat[:, i, :]), sem("dve_bn"))

    def rstd(i, add_square, ready):
        dve.wait(ready)
        src, bias = mv[:, i, 1:2], eps1
        if add_square:
            ready = stt(ms[:, i:i + 1], mv[:, i, 0:1], mv[:, i, 0:1], mv[:, i, 1:2], ALU.mult, ALU.add, sem("dve_ms"))
            src, bias = ms[:, i:i + 1], eps2
        act.wait(ready, c_eps)
        t = activate(rs[:, i:i + 1], src, ACT.Sqrt, sem("act_sqrt"), bias=bias[:, 0:1])
        dve.wait(t)
        return recip(rs[:, i:i + 1], rs[:, i:i + 1], sem("dve_rs"))

    def layernorm(dst, src, i, ready):
        t = rstd(i, False, stats(src, i, ready))
        dve.wait(t)
        return ts(dve, dst, src, mv[:, i, 0:1], rs[:, i:i + 1], ALU.subtract, ALU.mult, sem("dve_norm"))

    def rms_rows(i, gain, ready):
        t = rstd(i, True, stats(Z[:, i, :], i, ready))
        h = HR.next()
        dve.wait(t, *h.free)
        return h, stt(h.t[:, :], Z[:, i, :], rs[:, i:i + 1], gain, ALU.mult, ALU.mult, sem("dve_norm"))

    def to_features(row, bk, th, tl, i, ready, name, free=()):
        pe.wait(*bk.free, ready, c_ident)
        for k in range(KD):
            t = turn(bk.t[:, k * T:(k + 1) * T], row[:, k * 128:(k + 1) * 128], ident[0:T, 0:T],
                     sem("pe_turn") if k == KD - 1 else None)
        cs = slice(i * T, (i + 1) * T)
        bk.free = [split(bk.t[:, 0:KD * T].rearrange("p (k t) -> p k t", k=KD), th[:, :, cs], tl[:, :, cs], name, t, free)]
        return t, bk.free[0]

    def to_rows(yt, i, bk, ready):
        pe.wait(ready, *bk.free)
        for f in range(KD):
            t = turn(bk.t[0:T, f * 128:(f + 1) * 128], yt[:, f, i * T:(i + 1) * T], ident[:, :],
                     sem("pe_turn") if f == KD - 1 else None)
        return t

    xin = x.rearrange("b t d -> t b d")
    x1_dram = s_x1.rearrange("b t d -> t b d")
    q_src = [[(whole, kpn(Wq)[:, :, n * 128:(n + 1) * 128])] for n in range(NH)]
    wo_v = Wo.rearrange("(n p) f -> p n f", p=128)
    o_src = [[(whole, wo_v[:, 4 * u:4 * u + 4, f * 128:(f + 1) * 128])] for f in range(KD) for u in range(4)]
    xs = Stream(xring, q_src + o_src + q_src + o_src, 3)
    state = {"kv": None, "qo_free": [], "work_free": []}
    z_ready = {}
    done_x1 = []

    def norm_x(half):
        for i in range(HB):
            t = layernorm(X[:, i, :], X[:, i, :], half * HB + i, [x_ready[half * HB + i]])
            p, t = to_features(X[:, i, :], banks[4 + i % 2], XTh, XTl, i, t, "xt", state["qo_free"])
            yield
        state["xt"] = t

    def load_kv(c):
        src, wh, wl = (Wk, WKh, WKl) if c < 4 else (Wv, WVh, WVl)
        cs = slice(c % 4 * 256, (c % 4 + 1) * 256)
        r, tok = load_unit([(rows4, kpn(src)[:, :, cs])])
        act.wait(tok)
        h = activate(wh[:, :, cs], rows4(r.t), ACT.Copy, sem("act_kv"))
        dve.wait(h)
        r.free = [tt(dve, wl[:, :, cs], rows4(r.t), f32(wh[:, :, cs]), ALU.subtract, sem("dve_kv"))]
        state["kv"] = r.free[0]

    def project_q(half):
        for n in range(NH):
            w, ready = xs.next()
            bk = banks[n % 4]
            pe.wait(ready, state["xt"], *bk.free)
            for k in range(KD):
                t = mm3(bk.t[:, 0:HT], w.t[:, 0, k, :], w.t[:, 1, k, :], XTh[:, k, :], XTl[:, k, :],
                        k == 0, k == KD - 1, sem("pe_q"))
            w.free = [t]
            bk.free = [split(bk.t[:, 0:HT], QOh[:, n, :], QOl[:, n, :], "q", t, state["qo_free"])]
            yield
        state["q_pe"], state["q"] = t, bk.free[0]

    def ctx_load(b):
        act.wait(*craw.free)
        dma(act, craw.t[:, 0:2, :], ctx_in[b, 0:256, :].rearrange("(c p) d -> p c d", p=128), craw.sem)
        state["ctx", b] = dma(act, craw.t[0:S - 256, 2, :], ctx_in[b, 256:S, :], craw.sem)

    JB = Ring(banks[2:5])
    ct_ready, ct_free = {}, {}

    def ctx_turn(b):
        for k in range(2):
            bk = JB.next()
            pe.wait(state["ctx", b], c_ident, *bk.free)
            for c, (o, n) in enumerate(CH):
                t = turn(bk.t[:, o:o + n], craw.t[0:n, c, k * 128:(k + 1) * 128], ident[0:n, 0:n],
                         sem("pe_ct") if c == 2 else None)
            ct_ready[b] = split(bk.t[:, 0:S], CTh[b % 2][:, k, 0:S], CTl[b % 2][:, k, 0:S], "ct", t,
                                ct_free.get(b - 2, []))
            bk.free = [ct_ready[b]]
        craw.free = [t]

    def attention(half):
        b0 = half * HB
        SB = Ring(banks[0:2])
        BA, BB, OB = banks[5], banks[6], banks[7]
        k_ready, k_free = {}, [None] * NKV
        v_ready, v_free = {}, [[], []]
        mb_ready = {}
        for q in (act, dve, pool):
            q.wait(state["q_pe"])

        def project_k(b, g):
            bk, gs = JB.next(), slice(g * 128, (g + 1) * 128)
            pe.wait(ct_ready[b], state["kv"], *bk.free)
            for k in range(2):
                t = mm3(bk.t[:, 0:SP], WKh[:, k, gs], WKl[:, k, gs], CTh[b % 2][:, k, :], CTl[b % 2][:, k, :],
                        k == 0, k == 1, sem("pe_k"))
            k_ready[b, g] = split(bk.t[:, 0:SP], Kh[:, g, :], Kl[:, g, :], "k", t, [k_free[g]] if k_free[g] else [])
            bk.free = [k_ready[b, g]]
            ct_free[b] = [t]

        def project_v(b, hv, c):
            bk = JB.next()
            o, n = CH[c]
            vs = slice(hv * 512, (hv + 1) * 512)
            pe.wait(ct_ready[b], state["kv"], *bk.free)
            for k in range(2):
                t = mm3(bk.t[0:n, :], CTh[b % 2][:, k, o:o + n], CTl[b % 2][:, k, o:o + n], WVh[:, k, vs], WVl[:, k, vs],
                        k == 0, k == 1, sem("pe_v"))
            v_ready[b, hv] = split(bk.t[0:n, :], Vh[0:n, c, vs], Vl[0:n, c, vs], "v", t, v_free[hv])
            bk.free = [v_ready[b, hv]]
            ct_free[b] = [t]

        def scores(b, g):
            qs = slice((b - b0) * T, (b - b0 + 1) * T)
            sc, m = SC.next(), mx.next()
            if g == 0:
                mb_ready[b] = ts(dve, mb[:, :], mask8[:, b * S:(b + 1) * S], 1.0, BIG, ALU.subtract, ALU.mult, sem("dve_mb"))
            for h in range(2):
                bk = SB.next()
                pe.wait(k_ready[b, g], state["q"], *bk.free)
                t = mm3(bk.t[0:T, 0:SP], QOh[:, 2 * g + h, qs], QOl[:, 2 * g + h, qs], Kh[:, g, :], Kl[:, g, :],
                        True, True, sem("pe_s"))
                dve.wait(t, mb_ready[b], *sc.free, *m.free)
                o, a, acc = sc.t[:, h, :], bk.t[0:T, 0:S], m.t[:, 0, h:h + 1]
                t2 = dve.do(lambda e, o=o, a=a, acc=acc: e.tensor_tensor_reduce(
                    o, a, mb[:, :], 1.0, -3.0e38, ALU.add, ALU.max, acc), sem("dve_smax"))
                bk.free = [t2]
            k_free[g] = t
            dve.wait(t2)
            return sc, m, ts(dve, m.t[:, 1, :], m.t[:, 0, :], -XS, None, ALU.mult, s=sem("dve_nmx"))

        def exps(sc, m, t):
            act.wait(t)
            for h in range(2):
                t = activate(sc.t[:, h, :], sc.t[:, h, :], ACT.Exp, sem("act_exp"), bias=m.t[:, 1, h:h + 1],
                             scale=XS, accum_out=m.t[:, 2, h:h + 1])
            return t

        def normalise(sc, m, t, b):
            dve.wait(t)
            t = recip(m.t[:, 3, :], m.t[:, 2, :], sem("dve_rec"))
            pool.wait(t, c_any)
            for h in range(2):
                t = ts(pool, sc.t[:, h, :], sc.t[:, h, :], m.t[:, 3, h:h + 1], anyv[:, b:b + 1],
                       ALU.mult, ALU.mult, sem("pool_p"))
            m.free = [t]
            return sc, t

        def turn_p(p, t):
            pt = PT.next()
            pe.wait(t, *BA.free, *BB.free)
            for c, (o, n) in enumerate(CH):
                for h in range(2):
                    dst = BA.t[:, (2 * c + h) * T:(2 * c + h + 1) * T] if c < 2 else BB.t[0:n, h * T:(h + 1) * T]
                    tk = turn(dst, p.t[:, h, o:o + n], ident[0:T, 0:T], sem("pe_pt") if h == 1 and c > 0 else None)
                    if c == 1 and h == 1:
                        t_a = tk
            p.free = [tk]
            ph, pl = pt.t
            BA.free = [split(BA.t[:, 0:4 * T], ph[:, 0:2, :].rearrange("p a b -> p (a b)"),
                             pl[:, 0:2, :].rearrange("p a b -> p (a b)"), "pt", t_a, pt.free)]
            n = CH[2][1]
            BB.free = [split(BB.t[0:n, 0:2 * T], ph[0:n, 2, :], pl[0:n, 2, :], "pt", tk)]
            return pt, BB.free[0]

        def weighted(b, g, pt, t):
            ph, pl = pt.t
            gs = slice(g * 128, (g + 1) * 128)
            pe.wait(t, v_ready[b, g // 4], *OB.free)
            for c, (_, n) in enumerate(CH):
                tk = mm3(OB.t[:, 0:2 * T], Vh[0:n, c, gs], Vl[0:n, c, gs], ph[0:n, c, :], pl[0:n, c, :],
                         c == 0, c == 2, sem("pe_o"))
            pt.free = [tk]
            v_free[g // 4] = [tk]
            qs = slice((b - b0) * T, (b - b0 + 1) * T)
            src = OB.t[:, 0:2 * T].rearrange("p (h q) -> p h q", h=2)
            OB.free = [split(src, QOh[:, 2 * g:2 * g + 2, qs], QOl[:, 2 * g:2 * g + 2, qs], "o", tk)]
            return tk, OB.free[0]

        for g in range(NKV):
            project_k(b0, g)
        for c in range(3):
            project_v(b0, 0, c)
        steps = [(b, g) for b in range(b0, b0 + HB) for g in range(NKV)]
        soft, turned = {}, {}
        last = b0 + HB - 1
        for i in range(len(steps) + 3):
            live = i < len(steps)
            if live:
                b, g = steps[i]
                sc, m, t = scores(b, g)
            if 1 <= i <= len(steps):
                soft[i - 1] = normalise(*soft[i - 1])
            if 2 <= i <= len(steps) + 1:
                turned[i - 2] = turn_p(*soft.pop(i - 2))
            if live:
                soft[i] = sc, m, exps(sc, m, t), b
                if b < last:
                    project_k(b + 1, g)
                if 3 <= g <= 5:
                    project_v(b, 1, g - 3)
                if g == 1 and b > b0:
                    project_v(b, 0, 2)
            if i >= 3:
                state["o_pe"], state["o"] = weighted(*steps[i - 3], *turned.pop(i - 3))
            if live:
                if b < last and g >= 6:
                    project_v(b + 1, 0, g - 6)
                if g == 5 and b + 2 <= last:
                    ctx_turn(b + 2)
                    if b + 3 <= last:
                        ctx_load(b + 3)
                if i == len(steps) - 4:
                    xs.fill()

    def out_projection(half):
        act.wait(state["o_pe"])
        dve.wait(state["o_pe"])
        if half == 0:
            load_x(1)
            state["qo_free"] = []
        xr = dma(act, XR[:, :, :], xin[:, half * HB:(half + 1) * HB, :], sem("dma_xr"))
        for f in range(KD):
            bk = banks[f % 2]
            for u in range(4):
                w, ready = xs.next()
                pe.wait(ready, state["o"], *bk.free)
                for k in range(4):
                    t = mm3(bk.t[:, 0:HT], w.t[:, 0, k, :], w.t[:, 1, k, :], QOh[:, 4 * u + k, :], QOl[:, 4 * u + k, :],
                            u == 0 and k == 0, u == 3 and k == 3, sem("pe_wo"), k == 3)
                w.free = [t]
                if u == 3:
                    act.wait(t, *state.get("yt_free", []))
                    y = activate(YT[:, f, :], bk.t[:, 0:HT], ACT.Copy, sem("act_yt"))
                    bk.free = [y]
                yield
        state["qo_free"] = [t]
        state["y"], state["xr"] = y, xr

    def residual(half):
        for i in range(HB):
            b, bk = half * HB + i, banks[6 + i % 2]
            t = to_rows(YT, i, bk, state["y"])
            dve.wait(t, state["xr"], c_tanh)
            t2 = stt(XR[:, i, :], bk.t[0:T, :], tgx[:, 0:1], XR[:, i, :], ALU.mult, ALU.add, sem("dve_x1"))
            bk.free = [t2]
            z_ready[b] = layernorm(Z[:, b, :], XR[:, i, :], b, [t2])
            act.wait(t2)
            done_x1.append(dma(act, s_x1[b], XR[:, i, :], sem("dma_x1")))
            yield
        state["yt_free"] = [t]

    def drain(gen, n=10 ** 6):
        for _ in range(n):
            if next(gen, gen) is gen:
                return

    dve.wait(c_mask)
    c_any = reduce(anyv[:, :], mask8[:, :].rearrange("p (b s) -> p b s", s=S), ALU.max, sem("dve_any"))
    xs.fill()
    drain(norm_x(0))
    for ct in CTh + CTl:
        z = ct[:, :, S:SP]
        state["pad"] = pool.do(lambda e, z=z: e.memset(f32(z), 0.0), sem("pool_pad"))
    pe.wait(state["pad"])
    ctx_load(0)
    q = project_q(0)
    drain(q, 3)
    for c in range(8):
        load_kv(c)
        drain(q, 1)
    ctx_turn(0)
    ctx_load(1)
    drain(q, 3)
    ctx_turn(1)
    drain(q)
    ctx_load(2)
    attention(0)

    o = out_projection(0)
    drain(o, 6)
    nx = norm_x(1)
    for _ in range(HB):
        drain(nx, 1)
        drain(o, 2)
    drain(o)
    drain(nx)
    q = project_q(1)
    drain(q, 1)
    res = residual(0)
    ctx_load(4)
    for i in range(HB):
        drain(res, 1)
        drain(q, 1)
    drain(res)
    ctx_turn(4)
    ctx_load(5)
    drain(q, 4)
    ctx_turn(5)
    ctx_load(6)
    drain(q)
    for q_ in (act, dve, pool):
        q_.wait(state["yt_free"][0], done_x1[-1])
    attention(1)

    sq = kpn
    qk_src = [[(whole, sq(w)[:, :, m * 128:(m + 1) * 128])] for w in (wq, wk) for m in range(KD)]
    v_src = [[(whole, sq(wv)[:, :, m * 128:(m + 1) * 128])] for m in range(KD)]
    wo_src = [[(whole, sq(wo)[:, :, m * 128:(m + 1) * 128])] for m in range(KD)]
    dflat = w_down.rearrange("e i h -> (e i) h")

    def segments(grp, j):
        if grp == 0:
            return [(0, 128, NE, j * 128)]
        lo = (grp - 1) * 4 * EI + j * 128
        at, out_ = lo, []
        while at < lo + 128:
            e = at // EI
            end = min(lo + 128, (e + 1) * EI)
            out_.append((at - lo, end - at, e, at - e * EI))
            at = end
        return out_

    def up_units(grp, j):
        if grp == 0:
            return [[(whole, sq(w)[:, :, j * 128:(j + 1) * 128])] for w in (sh_gate, sh_up)]
        return [[(part(o, n), sq(w[e])[:, :, a:a + n]) for o, n, e, a in segments(grp, j)] for w in (w_gate, w_up)]

    def down_units(grp, f):
        base = sh_down if grp == 0 else dflat[(grp - 1) * 4 * EI:grp * 4 * EI, :]
        v = base.rearrange("(j p) f -> p j f", p=128)[:, :, f * 128:(f + 1) * 128]
        return [[((lambda t, n=n: t[:, 0:n, :]), v[:, a:a + n, :])] for a, n in ((0, 4), (4, 4), (8, 3))]

    N0 = 4
    s_up = [up_units(0, j) for j in range(NJ)]
    s_down = [u for f in range(KD) for u in down_units(0, f)]

    def flat(units):
        return [u for pair in units for u in pair]

    f_src = qk_src + v_src + v_src + qk_src + wo_src
    f_src += flat(s_up[:N0]) + wo_src + flat(s_up[N0:]) + s_down + flat(s_up) + s_down
    for grp in (1, 2):
        f_src += flat([up_units(grp, j) for j in range(NJ)])
        f_src += [u for f in range(KD) for u in down_units(grp, f)] * grp
    fs = Stream(fring, f_src, 4)
    DB = Ring(banks[5:8])
    ht_ready, qk_ready, v_tok, cx_ready, h2_ready = [[]] * 2, [None] * 2, [None] * 2, [None] * 2, [None] * 2

    def features(half, i, ready, bk):
        b = half * HB + i
        h, t = rms_rows(b, ln1b[:, :], [ready, state["ln1"]])
        p, t = to_features(h.t, bk, HTh[half], HTl[half], i, t, "ht")
        h.free = [p]
        ht_ready[half] = [t]

    def project_qk(h):
        for n in range(8):
            w, ready = fs.next()
            dst, bias = (QT[h], bqc) if n < 4 else (KT[h], bkc)
            m, bk = n % 4, DB.next()
            pe.wait(ready, *ht_ready[h], *bk.free)
            for k in range(KD):
                t = mm3(bk.t[:, 0:HT], w.t[:, 0, k, :], w.t[:, 1, k, :], HTh[h][:, k, :], HTl[h][:, k, :],
                        k == 0, k == KD - 1, sem("pe_qk"))
            w.free = [t]
            p = PQ.next()
            act.wait(t, state["c1"], *p.free)
            t2 = activate(p.t[:, 0, :], bk.t[:, 0:HT], ACT.Identity, sem("act_f"), bias=bias[:, m:m + 1])
            bk.free = [t2]
            dve.wait(t2)
            o, a = p.t[:, 1, :], p.t[:, 0, :]
            t3 = dve.do(lambda e, o=o, a=a: e.stream_shuffle(o, a, SWAP), sem("dve_shuf"))
            pool.wait(t2)
            q4 = lambda ap: ap.rearrange("p (b t) -> p b t", t=T)
            t4 = tt(pool, q4(p.t[:, 2, :]), q4(p.t[:, 0, :]), cosT[:, :, :], ALU.mult, sem("pool_cos"))
            dve.wait(t3)
            t5 = tt(dve, q4(p.t[:, 1, :]), q4(p.t[:, 1, :]), sinT[:, :, :], ALU.mult, sem("dve_sin"))
            pool.wait(t4, t5)
            qk_ready[h] = tt(pool, dst[:, m, :], p.t[:, 1, :], p.t[:, 2, :], ALU.add, sem("pool_rope"))
            p.free = [qk_ready[h]]
            yield
        state["qk_pe", h] = t

    def project_v_rows(h):
        for m in range(KD):
            w, ready = fs.next()
            for i in range(HB):
                bk = banks[i]
                pe.wait(ready, *ht_ready[h], *bk.free)
                ts_ = slice(i * T, (i + 1) * T)
                for k in range(KD):
                    t = mm3(bk.t[0:T, m * 128:(m + 1) * 128], HTh[h][:, k, ts_], HTl[h][:, k, ts_],
                            w.t[:, 0, k, :], w.t[:, 1, k, :], k == 0, k == KD - 1, sem("pe_fv"))
                if m == KD - 1:
                    dve.wait(t, state["c2"])
                    v_tok[h] = tt(dve, V[h][:, i, :], bk.t[0:T, :], bvb[:, :], ALU.add, sem("dve_v2"))
                    bk.free = [v_tok[h]]
            w.free = [t]
            yield

    def self_attention(h):
        FB, TB, OB = Ring(banks[0:2]), Ring(banks[2:3]), Ring(banks[3:5])

        def f_scores(b, i):
            bs, ps = slice(b * T, (b + 1) * T), slice(32 * i, 32 * i + 32)
            p, m, bk = PF.next(), sm.next(), FB.next()
            pe.wait(qk_ready[h], state["cb"], *bk.free)
            matmul(bk.t[0:T, 0:4 * T], identb[:, :], causb[:, :, :].rearrange("p a b -> p (a b)"), True, False)
            for c in range(4):
                t = matmul(bk.t[0:T, c * T:(c + 1) * T], QT[h][ps, c, bs], KT[h][ps, c, bs], False, c == 3,
                           sem("pe_fs") if c == 3 else None)
            dve.wait(t, *m.free)
            t = reduce(m.t[:, 0, :], bk.t[0:T, 0:4 * T].rearrange("p (a b) -> p a b", a=4), ALU.max, sem("dve_fm"))
            dve.wait(t)
            t = ts(dve, m.t[:, 1, :], m.t[:, 0, :], -FS, None, ALU.mult, s=sem("dve_fn"))
            act.wait(t, *p.free)
            for c in range(4):
                t = activate(p.t[:, c, :], bk.t[0:T, c * T:(c + 1) * T], ACT.Exp,
                             sem("act_fe") if c == 3 else None, bias=m.t[:, 1, c:c + 1], scale=FS,
                             accum_out=m.t[:, 2, c:c + 1])
            bk.free = [t]
            return p, m, t

        def f_norm(p, m, t):
            dve.wait(t)
            t = recip(m.t[:, 3, :], m.t[:, 2, :], sem("dve_fr"))
            dve.wait(t)
            r4 = m.t[:, 3, :].rearrange("p (a o) -> p a o", o=1).broadcast_to([T, 4, T])
            t = tt(dve, p.t[:, :, :], p.t[:, :, :], r4, ALU.mult, sem("dve_fp"))
            m.free = [t]
            return p, t

        def f_turn(i, p, t):
            pt, bk = PTf.next(), TB.next()
            pe.wait(t, *bk.free)
            for c in range(4):
                tk = turn(bk.t[0:T, c * T:(c + 1) * T], p.t[:, c, :], ident[0:T, 0:T], sem("pe_ft") if c == 3 else None)
            p.free = [tk]
            dst = pt.t[:, :, :].rearrange("p a b -> p (a b)")
            if i % 2:
                dve.wait(tk, *pt.free)
                t = copy(dve, dst, bk.t[0:T, 0:4 * T], sem("dve_ft"))
            else:
                act.wait(tk, *pt.free)
                t = activate(dst, bk.t[0:T, 0:4 * T], ACT.Copy, sem("act_ft"))
            bk.free = [t]
            return pt, t

        def f_out(b, i, pt, t):
            if i == 0:
                OB.next()
            bk = OB.slots[(OB.n - 1) % 2]
            pe.wait(t, v_tok[h], *bk.free)
            for c in range(4):
                hcol = (4 * c + i) * FD
                t = matmul(bk.t[32 * i:32 * i + 32, c * T:(c + 1) * T], V[h][:, b, hcol:hcol + FD],
                           pt.t[:, c, :], True, True, sem("pe_fo") if c == 3 else None)
            pt.free = [t]
            if i == 3:
                bs = slice(b * T, (b + 1) * T)
                src = bk.t[:, 0:4 * T].rearrange("p (a b) -> p a b", a=4)
                cx_ready[h] = split(src, CXh[h][:, :, bs], CXl[h][:, :, bs], "cx", t)
                bk.free = [cx_ready[h]]

        units = [(b, i) for b in range(HB) for i in range(4)]
        raised, normed, turned = {}, {}, {}
        for n in range(len(units) + 3):
            if n < len(units):
                raised[n] = f_scores(*units[n])
            if 1 <= n <= len(units):
                normed[n - 1] = f_norm(*raised.pop(n - 1))
            if 2 <= n <= len(units) + 1:
                turned[n - 2] = f_turn(units[n - 2][1], *normed.pop(n - 2))
            if n >= 3:
                f_out(*units[n - 3], *turned.pop(n - 3))
            yield

    def project_o(h):
        for m in range(KD):
            w, ready = fs.next()
            bk = DB.next()
            pe.wait(ready, cx_ready[h], *bk.free)
            for k in range(KD):
                t = mm3(bk.t[:, 0:HT], w.t[:, 0, k, :], w.t[:, 1, k, :], CXh[h][:, k, :], CXl[h][:, k, :],
                        k == 0, k == KD - 1, sem("pe_fo2"))
            w.free = [t]
            act.wait(t, *state["yt_free"])
            y = activate(YTf[:, m, :], bk.t[:, 0:HT], ACT.Copy, sem("act_yt"))
            bk.free = [y]
            yield
        state["y"], state["wo_pe", h] = y, t

    def epilogue(h):
        for q in (act, dve):
            q.wait(state["qk_pe", 1])
        for i in range(HB):
            b = h * HB + i
            bk = DB.next()
            t = to_rows(YTf, i, bk, state["y"])
            dve.wait(t)
            t2 = tt(dve, Z[:, b, :], bk.t[0:T, :], Z[:, b, :], ALU.add, sem("dve_x2"))
            bk.free = [t2]
            hr, t3 = rms_rows(b, ln2b[:, :], [t2, state["c2"]])
            yield
            p, h2_ready[h] = to_features(hr.t, DB.next(), H2h[h], H2l[h], i, t3, "h2")
            hr.free = [p]
        state["yt_free"] = [t]
        yield
        bk = DB.next()
        pe.wait(h2_ready[h], state["wr"], *bk.free)
        for i in range(HB):
            bs = slice(i * T, (i + 1) * T)
            for k in range(KD):
                t = mm3(bk.t[0:T, i * 10:i * 10 + 10], H2h[h][:, k, bs], H2l[h][:, k, bs], WRh[:, k, :], WRl[:, k, :],
                        k == 0, k == KD - 1, sem("pe_r"))
        sd = sem("dve_r")

        def link(t):
            dve.wait(t)

        def wide(i):
            return r1[:, i, :].rearrange("p (b o) -> p b o", o=1).broadcast_to([T, HB, NE])

        dve.wait(t, state["io"], *state.get("comb_free", []))
        t = copy(dve, L[:, :, :], bk.t[0:T, 0:HB * 10].rearrange("p (b n) -> p b n", n=10), sd)
        bk.free = [t]
        link(t)
        link(reduce(r1[:, 0, :], L[:, :, 0:NE], ALU.max, sd))
        t = tt(dve, pr[:, :, :], L[:, :, 0:NE], wide(0), ALU.subtract, sd)
        act.wait(t)
        t = activate(pr[:, :, :], pr[:, :, :], ACT.Exp, sem("act_r"))
        sg = activate(L[:, :, NE:NE + 1], L[:, :, NE:NE + 1], ACT.Tanh, sem("act_r"), scale=0.5)
        yield
        link(t)
        link(reduce(r1[:, 0, :], pr[:, :, :], ALU.add, sd))
        link(recip(r1[:, 1, :], r1[:, 0, :], sd))
        link(tt(dve, pr[:, :, :], pr[:, :, :], wide(1), ALU.mult, sd))
        src = pr
        for r, sl in ((0, sel1), (1, sel2)):
            link(reduce(r1[:, 2, :], src[:, :, :], ALU.max, sd))
            link(tt(dve, sl[:, :, :], src[:, :, :], wide(2), ALU.is_equal, sd))
            link(tt(dve, sl[:, :, :], sl[:, :, :], io8[:, :, :], ALU.mult, sd))
            link(reduce(r1[:, 3, :], sl[:, :, :], ALU.max, sd))
            link(tt(dve, sl[:, :, :], io8[:, :, :], wide(3), ALU.is_equal, sd))
            if r == 0:
                link(stt(w8[:, :, :], sl[:, :, :], -4.0, pr[:, :, :], ALU.mult, ALU.add, sd))
                src = w8
        link(tt(dve, sel1[:, :, :], sel1[:, :, :], sel2[:, :, :], ALU.add, sd))
        stt(comb[:, :, 0:NE], pr[:, :, :], 0.5, sel1[:, :, :], ALU.mult, ALU.mult, sd)
        dve.wait(sg)
        t = ts(dve, comb[:, :, NE:NE + 1], L[:, :, NE:NE + 1], 0.25, 0.25, ALU.mult, ALU.add, s=sd)
        yield
        bk = DB.next()
        pe.wait(t, *bk.free)
        for i in range(HB):
            tk = turn(bk.t[0:NE + 1, i * T:(i + 1) * T], comb[:, i, :], ident[0:T, 0:T],
                      sem("pe_turn") if i == HB - 1 else None)
        dve.wait(tk)
        ct = copy(dve, combT[:, :], bk.t[0:NE + 1, 0:HT], sem("dve_ct2"))
        bk.free = [ct]
        act.wait(ct)
        state["comb", h] = dma(act, s_comb[h], combT[:, :], sem("dma_comb"))
        state["comb_free"] = [state["comb", h]]

    hd_free, hd_ready, y_ready = [[], []], [{}, {}], [None, None]

    def up(grp, j, halves, MB):
        gates, banks_g, tms = [], [], []
        for h in halves:
            gt = G.next()
            sp.wait(state["comb", h], *gt.free)
            for o, n, e, _ in segments(grp, j):
                g_tok = dma(sp, gt.t[o:o + n, :], bass.AP(s_comb.tensor, (h * (NE + 1) + e) * HT, [[0, n], [1, HT]]), gt.sem)
            gates.append((gt, g_tok))

        def tile(w, ready, h, bk):
            pe.wait(ready, h2_ready[h], *bk.free)
            for k in range(KD):
                t = mm3(bk.t[:, 0:HT], w.t[:, 0, k, :], w.t[:, 1, k, :], H2h[h][:, k, :], H2l[h][:, k, :],
                        k == 0, k == KD - 1, sem("pe_gu"))
            return t

        w, ready = fs.next()
        for h in halves:
            bk, tm = MB.next(), TM.next()
            t = tile(w, ready, h, bk)
            act.wait(t, *tm.free)
            s_tok = activate(tm.t[:, 0, :], bk.t[:, 0:HT], ACT.Tanh, sem("act_th"), scale=0.5)
            dve.wait(s_tok)
            tok = stt(tm.t[:, 0, :], tm.t[:, 0, :], 1.0, bk.t[:, 0:HT], ALU.add, ALU.mult, sem("dve_silu"))
            bk.free = [tok]
            tms.append((tm, tok))
        w.free = [t]
        yield
        w, ready = fs.next()
        for h, (tm, tok), (gt, g_tok) in zip(halves, tms, gates):
            bk = MB.next()
            t = tile(w, ready, h, bk)
            dve.wait(t, tok)
            m_tok = tt(dve, tm.t[:, 0, :], bk.t[:, 0:HT], tm.t[:, 0, :], ALU.mult, sem("dve_gu"))
            bk.free = [m_tok]
            pool.wait(m_tok, g_tok)
            p_tok = tt(pool, tm.t[:, 1, :], tm.t[:, 0, :], gt.t[:, :], ALU.mult, sem("pool_gu"))
            gt.free = [p_tok]
            act.wait(p_tok, *hd_free[h])
            h_tok = activate(HDh[h][:, j, :], tm.t[:, 1, :], ACT.Copy, sem("act_hd"))
            dve.wait(h_tok)
            hd_tok = tt(dve, HDl[h][:, j, :], tm.t[:, 1, :], f32(HDh[h][:, j, :]), ALU.subtract, sem("dve_hd"))
            tm.free = [hd_tok]
            hd_ready[h][j] = [h_tok, hd_tok]
        w.free = [t]
        yield

    def down(grp, halves, MB):
        for f in range(KD):
            bks = [MB.next() for _ in halves]
            for a, n in ((0, 4), (4, 4), (8, 3)):
                w, ready = fs.next()
                for h, bk in zip(halves, bks):
                    pe.wait(ready, *bk.free)
                    for jj in range(n):
                        j = a + jj
                        pe.wait(*hd_ready[h][j])
                        t = mm3(bk.t[:, 0:HT], w.t[:, 0, jj, :], w.t[:, 1, jj, :], HDh[h][:, j, :], HDl[h][:, j, :],
                                j == 0, j == NJ - 1, sem("pe_d"), jj == n - 1)
                    if a == 8:
                        if grp == 0:
                            act.wait(t, *state["y_free"])
                            y_ready[h] = activate(Y[h][:, f, :], bk.t[:, 0:HT], ACT.Copy, sem("act_y"))
                        else:
                            dve.wait(t, y_ready[h])
                            y_ready[h] = tt(dve, Y[h][:, f, :], bk.t[:, 0:HT], Y[h][:, f, :], ALU.add, sem("dve_y"))
                        bk.free = [y_ready[h]]
                w.free = [t]
                yield
        for h in halves:
            hd_free[h] = [t]

    act.wait(state["o_pe"])
    dve.wait(state["o_pe"])
    pool.wait(state["o_pe"])
    for i in range(4):
        dma(act, cosT[:, i, :], c_cos, sem("dma_c1"))
        dma(act, sinT[:, i, :], c_sin, sem("dma_c1"))
    dma_columns(act, bqc[:, :], b_q.rearrange("(k p) -> p k", p=128), sem("dma_c1"))
    state["c1"] = dma_columns(act, bkc[:, :], b_k.rearrange("(k p) -> p k", p=128), sem("dma_c1"))
    state["ln1"] = dma(act, ln1b[:, :], bass.AP(w_ln1.tensor, 0, [[0, T], [1, D]]), sem("dma_ln1"))
    c_caus = dma(act, causal[:, :], c_causal, sem("dma_caus"))

    o = out_projection(1)
    drain(o, 4)
    fs.fill()
    for i in range(HB):
        features(0, i, z_ready[i], banks[4 + i % 2])
        drain(o, 3)
    drain(o)
    wo_done = state["qo_free"][0]
    for q in (act, dve, pool):
        q.wait(wo_done)
    for i in range(4):
        pool.wait(c_caus)
        copy(pool, causb[:, i, :], causal[:, :], sem("pool_cb"))
    state["cb"] = copy(pool, identb[:, :], ident[0:T, 0:T], sem("pool_cb"))
    dma(act, bvb[:, :], bass.AP(b_v.tensor, 0, [[0, T], [1, D]]), sem("dma_c2"))
    state["c2"] = dma(act, ln2b[:, :], bass.AP(w_ln2.tensor, 0, [[0, T], [1, D]]), sem("dma_c2"))
    z_tok = pool.do(lambda e: e.memset(WR[:, :, :], 0.0), sem("pool_wr"))
    for i in range(NE):
        zi = io8[:, :, i:i + 1]
        state["io"] = pool.do(lambda e, zi=zi, i=i: e.memset(zi, float(NE - i)), sem("pool_wr"))
    act.wait(z_tok)
    dma(act, WR[:, :, 0:NE], kpn(w_router), sem("dma_wr"))
    wt = dma_columns(act, WR[:, :, NE:NE + 1], kpn(sh_eg), sem("dma_wr"))

    qk = project_qk(0)
    drain(qk, 1)
    res = residual(1)
    for i in range(HB):
        drain(res, 1)
        drain(qk, 1)
        if i:
            features(1, i - 1, z_ready[HB + i - 1], banks[4 + i % 2])
    drain(res)
    drain(qk, 1)
    features(1, HB - 1, z_ready[B - 1], banks[4])
    pool.wait(wt)
    h = copy(pool, WRh[:, :, :], WR[:, :, :], sem("pool_wr"))
    pool.wait(h)
    state["wr"] = tt(pool, WRl[:, :, :], WR[:, :, :], f32(WRh[:, :, :]), ALU.subtract, sem("pool_wr"))
    drain(qk)
    drain(project_v_rows(0))
    drain(project_v_rows(1))
    qk, at0 = project_qk(1), self_attention(0)
    for _ in range(8):
        drain(at0, 2)
        drain(qk, 1)
    drain(qk)
    drain(at0)
    drain(project_o(0))
    at1, ep = self_attention(1), epilogue(0)
    for _ in range(8):
        drain(at1, 1)
        drain(ep, 1)
    drain(ep)
    for q in (act, dve, pool):
        q.wait(state["wo_pe", 0], qk_ready[1])
    state["y_free"] = [done_x1[-1]]

    def shared(h, MB, js):
        for j in js:
            yield from up(0, j, [h], MB)

    s0 = shared(0, DB, range(N0))
    for _ in range(8):
        drain(s0, 1)
        drain(at1, 1)
    drain(s0)
    drain(at1)
    drain(project_o(1))
    s0, ep = shared(0, DB, range(N0, NJ)), epilogue(1)
    for _ in range(8):
        drain(ep, 1)
        drain(s0, 1)
    drain(ep)
    drain(s0)
    MB = Ring(banks)
    drain(down(0, [0], MB))
    for q in (act, dve):
        q.wait(state["wo_pe", 1])
    drain(shared(1, MB, range(NJ)))
    drain(down(0, [1], MB))

    def add_x1():
        for b in range(B):
            r = HR.next()
            sp.wait(*r.free)
            t = dma(sp, r.t[:, :], s_x1[b], sem(f"dma_hr{b % 2}"))
            dve.wait(t)
            t = stt(Z[:, b, :], Z[:, b, :], tgf[:, 0:1], r.t[:, :], ALU.mult, ALU.add, sem("dve_zf"))
            r.free = [t]
            yield
        state["zf"] = t

    def result(h, i):
        b, bk, o = h * HB + i, MB.next(), OUT.next()
        t = to_rows(Y[h], i, bk, y_ready[h])
        dve.wait(t, state["zf"], *o.free)
        t = stt(o.t[:, :], bk.t[0:T, :], tgf[:, 0:1], Z[:, b, :], ALU.mult, ALU.add, sem("dve_out"))
        bk.free = [t]
        act.wait(t)
        o.free = [dma(act, out[b], o.t[:, :], o.sem)]

    zf = add_x1()
    for grp in (1, 2):
        for j in range(NJ):
            drain(up(grp, j, [0, 1], MB))
            drain(zf, 1)
        if grp == 1:
            drain(zf)
            drain(down(1, [0, 1], MB))
    drain(down(2, [0], MB))
    d1 = down(2, [1], MB)
    drain(d1, 1)
    for i in range(HB):
        result(0, i)
        drain(d1, 1)
    drain(d1)
    for i in range(HB):
        result(1, i)
    act.wait(*[tok for o in OUT.slots for tok in o.free])
    sp.wait(*done_x1, state["comb", 0], state["comb", 1])

    with top:
        block = top.enter_context(nc.Block())

        @block.sync
        def _(eng):
            sp.play(eng)

        @block.scalar
        def _(eng):
            act.play(eng)

        @block.vector
        def _(eng):
            dve.play(eng)

        @block.gpsimd
        def _(eng):
            pool.play(eng)

        @block.tensor
        def _(eng):
            pe.play(eng)


_INS = ['x', 'ctx_1024', 'mask_BxS2_bf1', 'g_xattn', 'g_ffn', 'L0_xattn_Wq', 'L0_xattn_Wk', 'L0_xattn_Wv',
        'L0_xattn_Wo', 'L0_ffn_w_ln1', 'L0_ffn_wq', 'L0_ffn_bq', 'L0_ffn_wk', 'L0_ffn_bk', 'L0_ffn_wv',
        'L0_ffn_bv', 'L0_ffn_wo', 'L0_ffn_w_ln2', 'L0_ffn_w_router', 'L0_ffn_w_gate_e', 'L0_ffn_w_up_e',
        'L0_ffn_w_down_e', 'L0_ffn_w_sh_gate', 'L0_ffn_w_sh_up', 'L0_ffn_w_sh_down', 'L0_ffn_w_sh_eg']


def _constants():
    ident = np.eye(128, dtype=np.float32)
    causal = np.where(np.tril(np.ones((T, T), bool)), np.float32(0), np.float32(-BIG)).astype(np.float32)
    inv = (np.float32(1.0) / np.power(np.float32(1.0e6), np.arange(0, FD, 2, dtype=np.float32) / np.float32(FD))).astype(np.float32)
    ang = (np.arange(T, dtype=np.float32)[:, None] * inv[None, :]).astype(np.float32)
    emb = np.concatenate([ang, ang], axis=-1)
    cos = np.cos(emb).astype(np.float32).T
    sin = np.sin(emb).astype(np.float32).T
    sin = np.concatenate([-sin[:FD // 2], sin[FD // 2:]], axis=0)
    return {'c_id': ident, 'c_causal': causal, 'c_cos': np.ascontiguousarray(np.tile(cos, (4, 1))),
            'c_sin': np.ascontiguousarray(np.tile(sin, (4, 1)))}


def kernel(**inputs):
    import numpy as _np
    import concourse.bacc as _bacc
    from concourse import mybir as _mybir
    from concourse.bass_utils import run_bass_kernel_spmd as _run

    nc = _bacc.Bacc("TRN2", target_bir_lowering=False, num_devices=1)
    arrays, args = {}, []
    for name in _INS:
        a = _np.ascontiguousarray(inputs[name])
        if a.dtype == _np.bool_:
            a = a.view(_np.uint8)
        arrays[f"in_{name}_dram"] = a
        args.append(nc.dram_tensor(f"in_{name}_dram", a.shape, _mybir.dt.from_np(a.dtype), kind="ExternalInput").ap())
    for name, a in _constants().items():
        arrays[f"in_{name}_dram"] = a
        args.append(nc.dram_tensor(f"in_{name}_dram", a.shape, _mybir.dt.from_np(a.dtype), kind="ExternalInput").ap())
    for name, shape in (("s_x1", (B, T, D)), ("s_x2", (B, T, D)), ("s_comb", (2, NE + 1, HT))):
        args.append(nc.dram_tensor(name, shape, F, kind="Internal").ap())
    args.append(nc.dram_tensor("out_0_dram", (B, T, D), F, kind="ExternalOutput").ap())
    flamingo_kernel(nc, *args)
    r = _run(nc, [arrays], core_ids=[0])
    return r.results[0]["out_0_dram"]
```

```python
from contextlib import ExitStack
from itertools import chain

import numpy as np
import concourse.bass as bass
from concourse import mybir

F = mybir.dt.float32
R = mybir.dt.float32r
BF = mybir.dt.bfloat16
U8 = mybir.dt.uint8
ALU = mybir.AluOpType
ACT = mybir.ActivationFunctionType
AX = mybir.AxisListType.X

B, T, D = 8, 100, 512
S, C = 361, 256
SP = 362
NH, NKV, HD = 16, 8, 128
FH, FD = 16, 32
NE, EI = 8, 352
HB = 4
HT = HB * T
TT = B * T
KD = D // 128
CH = [(0, 128), (128, 128), (256, S - 256)]
NJ = 11
BIG = 1.0e30
SB_START = 16512
SB_END = 229344
XS = float(1.0 / np.sqrt(np.float32(HD)))
FS = float(FD) ** -0.5
SWAP = [(i + 16) % 32 for i in range(32)]


class Sem:

    def __init__(self, handle):
        self.handle = handle
        self.count = 0

    def after(self, step):
        self.count += step
        return (self, self.count)


class Queue:

    def __init__(self):
        self.items = []
        self.seen = {}

    def wait(self, *tokens):
        for sem, value in tokens:
            if self.seen.get(sem, 0) < value:
                self.seen[sem] = value
                self.items.append((sem.handle, value, None))

    def do(self, emit, sem=None, step=1):
        self.items.append((sem.handle if sem else None, step, emit))
        return sem.after(step) if sem else None

    def play(self, eng):
        for handle, n, emit in self.items:
            if emit is None:
                eng.wait_ge(handle, n)
            elif handle is None:
                emit(eng)
            else:
                emit(eng).then_inc(handle, n)


class Region:

    def __init__(self, nc, start, end=SB_END):
        self.nc, self.at, self.end = nc, start, end

    def place(self, name, shape, dt=F):
        n = int(np.prod(shape[1:])) * {F: 4, R: 4, BF: 2, U8: 1}[dt]
        t = self.nc.alloc_sbuf_tensor_at(name, shape, dt, offset=self.at)
        self.at += (n + 31) // 32 * 32
        assert self.at <= self.end, (name, self.at, self.end)
        return t


class Slot:

    def __init__(self, t, sem=None):
        self.t = t
        self.sem = sem
        self.free = []


class Ring:
    def __init__(self, slots):
        self.slots = slots
        self.n = 0

    def next(self):
        self.n += 1
        return self.slots[(self.n - 1) % len(self.slots)]


def f32(ap):
    return ap.bitcast(F)


def flamingo_kernel(nc, x, ctx_in, mask, g_x, g_f, Wq, Wk, Wv, Wo, w_ln1, wq, b_q, wk, b_k, wv, b_v, wo,
                    w_ln2, w_router, w_gate, w_up, w_down, sh_gate, sh_up, sh_down, sh_eg,
                    c_id, c_causal, c_cos, c_sin, s_x1, s_comb, out):
    top = ExitStack()
    pe, act, dve, pool, sp = Queue(), Queue(), Queue(), Queue(), Queue()
    names = {}

    def sem(name):
        if name not in names:
            names[name] = Sem(top.enter_context(nc.semaphore(name)))
        return names[name]

    def matmul(o, a, b, start, stop, s=None):
        return pe.do(lambda e: e.matmul(o, a, b, start=start, stop=stop, skip_group_check=True), s)

    def mm3(o, ah, al, bh, bl, first, last, s=None, mark=None):
        matmul(o, ah, bh, first, False)
        matmul(o, ah, bl, False, False)
        return matmul(o, al, bh, False, last, s if (last if mark is None else mark) else None)

    def turn(o, i, ident, s=None):
        return pe.do(lambda e: e.transpose(o, i, ident), s)

    def activate(o, i, func, s=None, **kw):
        return act.do(lambda e: e.activation(o, i, func, **kw), s)

    def tt(q, o, a, b, op, s=None):
        return q.do(lambda e: e.tensor_tensor(o, a, b, op), s)

    def ts(q, o, a, s1, s2, op0, op1=None, s=None):
        if op1 is None:
            return q.do(lambda e: e.tensor_scalar(o, a, s1, None, op0), s)
        return q.do(lambda e: e.tensor_scalar(o, a, s1, s2, op0, op1), s)

    def stt(o, a, sc, b, op0, op1, s=None):
        return dve.do(lambda e: e.scalar_tensor_tensor(out=o, in0=a, scalar=sc, in1=b, op0=op0, op1=op1), s)

    def copy(q, o, i, s=None):
        return q.do(lambda e: e.tensor_copy(o, i), s)

    def reduce(o, i, op, s=None):
        return dve.do(lambda e: e.tensor_reduce(o, i, AX, op), s)

    def recip(o, i, s=None):
        return dve.do(lambda e: e.reciprocal(o, i), s)

    def dma(q, o, i, s):
        return q.do(lambda e: e.dma_start(o, i), s, 16)

    def dma_columns(q, o, i, s):
        return q.do(lambda e: e.dma_start(o, i, allow_slow_non_contiguous=True), s, 16)

    def split(src, hi, lo, name, ready, free=(), scale=None):
        act.wait(ready, *free)
        if scale is None:
            h = activate(hi, src, ACT.Copy, sem("act_" + name))
            dve.wait(h)
            return tt(dve, lo, src, f32(hi), ALU.subtract, sem("dve_" + name))
        h = activate(hi, src, ACT.Copy, sem("act_" + name), scale=scale)
        dve.wait(h)
        return stt(lo, src, scale, f32(hi), ALU.mult, ALU.subtract, sem("dve_" + name))

    banks = [Slot(top.enter_context(nc.psum_tensor(f"bank{i}", [128, 512], F))) for i in range(8)]

    P_ = Region(nc, SB_START)
    ident = P_.place("ident", [128, 128])
    mask8 = P_.place("mask8", [T, B * S], U8)
    anyv = P_.place("anyv", [T, B])
    gx = P_.place("gx", [T, 1])
    gf = P_.place("gf", [T, 1])
    tgx = P_.place("tgx", [T, 1])
    tgf = P_.place("tgf", [T, 1])
    stat = P_.place("stat", [T, B, 6])
    mv = P_.place("mv", [T, B, 2])
    rs = P_.place("rs", [T, B])
    ms = P_.place("ms", [T, B])
    mvz = P_.place("mvz", [T, B, 2])
    rz = P_.place("rz", [T, B])
    cosT = P_.place("cosT", [128, 1, T])
    sinT = P_.place("sinT", [128, 1, T])
    bqc = P_.place("bqc", [128, KD])
    bkc = P_.place("bkc", [128, KD])
    causb = P_.place("causb", [T, 1, T], BF)
    identb = P_.place("identb", [T, T], BF)
    eps1 = P_.place("eps1", [T, 1])
    eps2 = P_.place("eps2", [T, 1])
    raw = Ring([Slot(P_.place(f"raw{i}", [128, 4, 128]), sem(f"dma_raw{i}")) for i in range(4)])
    Z = P_.place("Z", [T, B, D])
    ffn0 = P_.at

    WKh = P_.place("WKh", [128, 2, NKV * 128], R)
    WKl = P_.place("WKl", [128, 2, NKV * 128], R)
    WVh = P_.place("WVh", [128, 2, NKV * 128], R)
    WVl = P_.place("WVl", [128, 2, NKV * 128], R)
    QOh = P_.place("QOh", [128, NH, HT], R)
    QOl = P_.place("QOl", [128, NH, HT], R)
    CTh = [P_.place(f"CTh{i}", [128, 2, SP], R) for i in range(2)]
    CTl = [P_.place(f"CTl{i}", [128, 2, SP], R) for i in range(2)]
    mb = P_.place("mb", [T, S])
    craw = Slot(P_.place("craw", [128, 3, C]), sem("dma_craw"))
    xring = Ring([Slot(P_.place(f"wx{i}", [128, 2, 4, 128], R)) for i in range(4)])
    work0 = P_.at

    A_ = Region(nc, work0)
    Kh = A_.place("Kh", [128, NKV, SP], R)
    Kl = A_.place("Kl", [128, NKV, SP], R)
    Vh = A_.place("Vh", [128, 3, NKV * 128], R)
    Vl = A_.place("Vl", [128, 3, NKV * 128], R)
    PT = Ring([Slot((A_.place(f"PTh{i}", [128, 3, 2 * T], R), A_.place(f"PTl{i}", [128, 3, 2 * T], R)))
               for i in range(2)])
    SC = Ring([Slot(A_.place(f"SC{i}", [T, 2, S])) for i in range(3)])
    mx = Ring([Slot(A_.place(f"mx{i}", [T, 4, 2])) for i in range(3)])

    C_ = Region(nc, work0)
    YT = C_.place("YT", [128, KD, HT])
    XR = C_.place("XR", [T, HB, D])
    X = C_.place("X", [T, HB, D])
    XTh = C_.place("XTh", [128, KD, HT], R)
    XTl = C_.place("XTl", [128, KD, HT], R)

    F_ = Region(nc, ffn0, work0)
    HTh = [F_.place(f"HTh{h}", [128, KD, HT], R) for h in range(2)]
    HTl = [F_.place(f"HTl{h}", [128, KD, HT], R) for h in range(2)]
    mid0 = F_.at
    QT, KT, V, CXh, CXl = ([None, None] for _ in range(5))

    def place_half(h):
        QT[h] = F_.place(f"QT{h}", [128, KD, HT])
        KT[h] = F_.place(f"KT{h}", [128, KD, HT])
        V[h] = F_.place(f"V{h}", [T, HB, D])
        CXh[h] = F_.place(f"CXh{h}", [128, KD, HT], R)
        CXl[h] = F_.place(f"CXl{h}", [128, KD, HT], R)

    place_half(0)
    PQ = Ring([Slot(F_.place(f"PQ{i}", [128, 3, HT])) for i in range(2)])
    half1 = F_.at
    place_half(1)
    bvb = F_.place("bvb", [T, D])
    after1 = F_.at
    ln2b = F_.place("ln2b", [T, D])
    sm = Ring([Slot(F_.place(f"sm{i}", [T, 4, 4])) for i in range(4)])
    WR = F_.place("WR", [128, KD, 10])
    WRh = F_.place("WRh", [128, KD, 10], R)
    WRl = F_.place("WRl", [128, KD, 10], R)
    L = F_.place("L", [T, HB, 10])
    pr = F_.place("pr", [T, HB, NE])
    w8 = F_.place("w8", [T, HB, NE])
    sel1 = F_.place("sel1", [T, HB, NE])
    sel2 = F_.place("sel2", [T, HB, NE])
    io8 = F_.place("io8", [T, HB, NE])
    r1 = F_.place("r1", [T, 4, HB])
    comb = F_.place("comb", [T, HB, NE + 1])
    LT = F_.place("LT", [10, HT])
    combT = F_.place("combT", [NE + 1, HT])

    E_ = Region(nc, work0 + 4 * (KD * HT + HB * D))
    ln1b = E_.place("ln1b", [T, D])
    HR = Ring([Slot(E_.place(f"HR{i}", [T, D])) for i in range(3)])
    fring = Ring([Slot(E_.place(f"wf{i}", [128, 2, 4, 128], R)) for i in range(6)])
    y1 = E_.at
    PF = Ring([Slot(E_.place(f"PF{i}", [T, 4, T])) for i in range(4)])
    PTf = Ring([Slot(E_.place(f"PTf{i}", [T, 4, T])) for i in range(3)])
    G = Ring([Slot(E_.place(f"G{i}", [128, HT]), sem(f"dma_g{i}")) for i in range(4)])
    YTf = Region(nc, work0).place("YTf", [128, KD, HT])

    H2 = Region(nc, ffn0, mid0)
    H2h = [H2.place(f"H2h{h}", [128, KD, HT], R) for h in range(2)]
    H2l = [H2.place(f"H2l{h}", [128, KD, HT], R) for h in range(2)]
    D0 = Region(nc, mid0, half1)
    D1 = Region(nc, half1, after1)
    HDh = [D0.place("HDh0", [128, NJ, HT], R), D1.place("HDh1", [128, NJ, HT], R)]
    HDl = [D0.place("HDl0", [128, NJ, HT], R), D1.place("HDl1", [128, NJ, HT], R)]
    TM = Ring([Slot(D0.place(f"TM{i}", [128, 2, HT])) for i in range(2)])
    Y_ = Region(nc, work0 + 4 * KD * HT, work0 + 4 * (KD * HT + HB * D))
    Y = [Y_.place("Y0", [128, KD, HT]), Region(nc, y1).place("Y1", [128, KD, HT])]
    OUT = Ring([Slot(o, sem(f"dma_out{i}")) for i, o in
                enumerate([Region(nc, ffn0 + i * 4 * D).place(f"OUT{i}", [T, D]) for i in range(4)])])
    x_ready = {}

    def load_x(half, queues):
        for i in range(HB):
            b = half * HB + i
            x_ready[b] = dma(queues[i % len(queues)], X[:, i, :], x[b], sem(f"dma_x{i}"))

    load_x(0, [act, sp])
    c_ident = dma(act, ident[:, :], c_id, sem("dma_ident"))
    pool.do(lambda e: e.memset(eps1[:, :], 1e-5), sem("pool_eps"))
    c_eps = pool.do(lambda e: e.memset(eps2[:, :], 1e-6), sem("pool_eps"))

    def load_constants():
        dma(act, gx[:, :], bass.AP(g_x.tensor, 0, [[0, T], [1, 1]]), sem("dma_c"))
        dma(act, gf[:, :], bass.AP(g_f.tensor, 0, [[0, T], [1, 1]]), sem("dma_c"))
        dma(act, mask8[:, :], bass.AP(mask.tensor, 0, [[0, T], [1, B * S]]), sem("dma_c"))
        dma(act, Z[:, 0, 0:T], c_causal, sem("dma_c"))
        dma(act, cosT[:, 0, :], c_cos, sem("dma_c"))
        dma(act, sinT[:, 0, :], c_sin, sem("dma_c"))
        dma_columns(act, bqc[:, :], b_q.rearrange("(k p) -> p k", p=128), sem("dma_c"))
        return dma_columns(act, bkc[:, :], b_k.rearrange("(k p) -> p k", p=128), sem("dma_c"))

    def whole(t):
        return t[:, :, :]

    def part(o, n):
        return lambda t: t[:, :, o:o + n]

    def flat_cols(t):
        return t[:, :, :].rearrange("p a b -> p (a b)")

    def rows4(t):
        return t[:, :, :].rearrange("p a b -> p (a b)").rearrange("p (k n) -> p k n", k=2)

    def kpn(w):
        return w.rearrange("(k p) n -> p k n", p=128)

    def load_unit(pieces):
        r = raw.next()
        sp.wait(*r.free)
        for view, src in pieces:
            tok = dma(sp, view(r.t), src, r.sem)
        return r, tok

    class Stream:

        def __init__(self, ring, sources, ahead):
            self.ring, self.sources, self.ahead, self.ready = ring, list(sources), ahead, []
            self.n, self.on_dve = 0, lambda n: False

        def fetch(self):
            if not self.sources:
                return
            r, tok = load_unit(self.sources.pop(0))
            w = self.ring.next()
            act.wait(tok, *w.free)
            h = activate(w.t[:, 0, :, :], r.t[:, :, :], ACT.Copy, sem("act_w"))
            q = dve if self.on_dve(self.n) else pool
            self.n += 1
            q.wait(h)
            lo = tt(q, w.t[:, 1, :, :], r.t[:, :, :], f32(w.t[:, 0, :, :]), ALU.subtract,
                    sem("dve_w" if q is dve else "pool_w"))
            r.free = [lo]
            self.ready.append((w, lo))

        def fill(self):
            while self.sources and len(self.ready) < self.ahead:
                self.fetch()

        def next(self):
            self.fetch()
            return self.ready.pop(0)

        def take(self, n):
            units, self.ready = self.ready[:n], self.ready[n:]
            return units

    def stats(row, m, i, ready):
        dve.wait(*ready)
        t = dve.do(lambda e: e.bn_stats(stat[:, i, :], row), sem("dve_bn"))
        dve.wait(t)
        return dve.do(lambda e: e.bn_aggr(m[:, i, :], stat[:, i, :]), sem("dve_bn"))

    def root(i, ready):
        act.wait(ready, c_eps)
        return activate(rs[:, i:i + 1], mv[:, i, 1:2], ACT.Sqrt, sem("act_sqrt"), bias=eps1[:, 0:1])

    def mean_square(i, ready):
        t = stats(Z[:, i, :], mvz, i, ready)
        dve.wait(t)
        return stt(ms[:, i:i + 1], mvz[:, i, 0:1], mvz[:, i, 0:1], mvz[:, i, 1:2], ALU.mult, ALU.add, sem("dve_ms"))

    def root_square(i, ready):
        act.wait(ready, c_eps)
        return activate(rz[:, i:i + 1], ms[:, i:i + 1], ACT.Sqrt, sem("act_sqrt"), bias=eps2[:, 0:1])

    def layernorm(dst, src, i, ready):
        dve.wait(ready)
        t = recip(rs[:, i:i + 1], rs[:, i:i + 1], sem("dve_rs"))
        dve.wait(t)
        return ts(dve, dst, src, mv[:, i, 0:1], rs[:, i:i + 1], ALU.subtract, ALU.mult, sem("dve_norm"))

    def rms_rows(i, gain, ready, inverse=True):
        h = HR.next()
        if not inverse:
            dve.wait(*ready, *h.free)
            return h, stt(h.t[:, :], Z[:, i, :], rz[:, i:i + 1], gain, ALU.mult, ALU.mult, sem("dve_rms"))
        dve.wait(ready[0])
        t = recip(rz[:, i:i + 1], rz[:, i:i + 1], sem("dve_rs"))
        act.wait(t, *h.free)
        t = activate(h.t[:, :], Z[:, i, :], ACT.Copy, sem("act_rms"), scale=rz[:, i:i + 1])
        pool.wait(t, ready[1])
        return h, tt(pool, h.t[:, :], h.t[:, :], gain, ALU.mult, sem("pool_rms"))

    def to_features(row, bk, th, tl, i, ready, name, free=()):
        pe.wait(*bk.free, ready, c_ident)
        for k in range(KD):
            t = turn(bk.t[:, k * T:(k + 1) * T], row[:, k * 128:(k + 1) * 128], ident[0:T, 0:T],
                     sem("pe_turn") if k == KD - 1 else None)
        cs = slice(i * T, (i + 1) * T)
        bk.free = [split(bk.t[:, 0:KD * T].rearrange("p (k t) -> p k t", k=KD), th[:, :, cs], tl[:, :, cs], name, t, free)]
        return t, bk.free[0]

    def to_rows(yt, i, bk, ready):
        pe.wait(ready, *bk.free)
        for f in range(KD):
            t = turn(bk.t[0:T, f * 128:(f + 1) * 128], yt[:, f, i * T:(i + 1) * T], ident[:, :],
                     sem("pe_turn") if f == KD - 1 else None)
        return t

    xin = x.rearrange("b t d -> t b d")
    x1_dram = s_x1.rearrange("b t d -> t b d")
    q_src = [[(whole, kpn(Wq)[:, :, n * 128:(n + 1) * 128])] for n in range(NH)]
    wo_v = Wo.rearrange("(n p) f -> p n f", p=128)
    o_src = [[(whole, wo_v[:, 4 * u:4 * u + 4, f * 128:(f + 1) * 128])] for u in range(4) for f in range(KD)]
    xs = Stream(xring, q_src + o_src + q_src + o_src, 3)
    state = {"kv": None, "qo_free": [], "work_free": []}
    z_ready = {}
    done_x1 = []

    def norm_x(half):
        roots, normed = {}, {}
        for i in range(HB + 2):
            if i < HB:
                b = half * HB + i
                roots[i] = root(b, stats(X[:, i, :], mv, b, [x_ready[b]]))
            if 1 <= i <= HB:
                normed[i - 1] = layernorm(X[:, i - 1, :], X[:, i - 1, :], half * HB + i - 1, roots[i - 1])
            if i >= 2:
                _, state["xt"] = to_features(X[:, i - 2, :], banks[4 + i % 2], XTh, XTl, i - 2, normed[i - 2], "xt",
                                             state["qo_free"])
            yield

    def load_kv(c):
        src, wh, wl = (Wk, WKh, WKl) if c < 4 else (Wv, WVh, WVl)
        cs = slice(c % 4 * 256, (c % 4 + 1) * 256)
        r, tok = load_unit([(rows4, kpn(src)[:, :, cs])])
        act.wait(tok)
        h = activate(wh[:, :, cs], rows4(r.t), ACT.Copy, sem("act_kv"))
        dve.wait(h)
        r.free = [tt(dve, wl[:, :, cs], rows4(r.t), f32(wh[:, :, cs]), ALU.subtract, sem("dve_kv"))]
        state["kv"] = r.free[0]

    def project_q(half):
        for n in range(NH):
            w, ready = xs.next()
            bk = banks[n % 4]
            pe.wait(ready, state["xt"], *bk.free)
            for k in range(KD):
                t = mm3(bk.t[:, 0:HT], w.t[:, 0, k, :], w.t[:, 1, k, :], XTh[:, k, :], XTl[:, k, :],
                        k == 0, k == KD - 1, sem("pe_q"))
            w.free = [t]
            bk.free = [split(bk.t[:, 0:HT], QOh[:, n, :], QOl[:, n, :], "q", t, state["qo_free"])]
            yield
        state["q_pe"], state["q"] = t, bk.free[0]

    def ctx_load(b):
        act.wait(*craw.free)
        dma(act, craw.t[:, 0:2, :], ctx_in[b, 0:256, :].rearrange("(c p) d -> p c d", p=128), craw.sem)
        state["ctx", b] = dma(act, craw.t[0:S - 256, 2, :], ctx_in[b, 256:S, :], craw.sem)

    JB = Ring(banks[2:5])
    ct_ready, ct_free = {}, {}

    def ctx_turn(b):
        for k in range(2):
            bk = JB.next()
            pe.wait(state["ctx", b], c_ident, *bk.free)
            for c, (o, n) in enumerate(CH):
                t = turn(bk.t[:, o:o + n], craw.t[0:n, c, k * 128:(k + 1) * 128], ident[0:n, 0:n],
                         sem("pe_ct") if c == 2 else None)
            ct_ready[b] = split(bk.t[:, 0:S], CTh[b % 2][:, k, 0:S], CTl[b % 2][:, k, 0:S], "ct", t,
                                ct_free.get(b - 2, []))
            bk.free = [ct_ready[b]]
        craw.free = [t]

    def wo_unit(u, f):
        bk = banks[(f + 2) % 4]
        w, ready = xs.next()
        pe.wait(ready, state["o", 2 * u + 1], *bk.free)
        for k in range(4):
            t = mm3(bk.t[:, 0:HT], w.t[:, 0, k, :], w.t[:, 1, k, :], QOh[:, 4 * u + k, :], QOl[:, 4 * u + k, :],
                    u == 0 and k == 0, u == 3 and k == 3, sem("pe_wo"), k == 3)
        w.free = [t]
        return bk, t

    def attention(half):
        b0 = half * HB
        SB = Ring(banks[0:2])
        BA, BB, OB = banks[5], banks[6], banks[7]
        k_ready, k_free = {}, [None] * NKV
        v_ready, v_free = {}, [[], []]
        mb_ready = {}
        for q in (act, dve, pool):
            q.wait(state["q_pe"])

        def project_k(b, g):
            bk, gs = JB.next(), slice(g * 128, (g + 1) * 128)
            pe.wait(ct_ready[b], state["kv"], *bk.free)
            for k in range(2):
                t = mm3(bk.t[:, 0:SP], WKh[:, k, gs], WKl[:, k, gs], CTh[b % 2][:, k, :], CTl[b % 2][:, k, :],
                        k == 0, k == 1, sem("pe_k"))
            k_ready[b, g] = split(bk.t[:, 0:SP], Kh[:, g, :], Kl[:, g, :], "k", t, [k_free[g]] if k_free[g] else [])
            bk.free = [k_ready[b, g]]
            ct_free[b] = [t]

        def project_v(b, hv, c):
            bk = JB.next()
            o, n = CH[c]
            vs = slice(hv * 512, (hv + 1) * 512)
            pe.wait(ct_ready[b], state["kv"], *bk.free)
            for k in range(2):
                t = mm3(bk.t[0:n, :], CTh[b % 2][:, k, o:o + n], CTl[b % 2][:, k, o:o + n], WVh[:, k, vs], WVl[:, k, vs],
                        k == 0, k == 1, sem("pe_v"))
            v_ready[b, hv] = split(bk.t[0:n, :], Vh[0:n, c, vs], Vl[0:n, c, vs], "v", t, v_free[hv])
            bk.free = [v_ready[b, hv]]
            ct_free[b] = [t]

        def scores(b, g):
            qs = slice((b - b0) * T, (b - b0 + 1) * T)
            sc, m = SC.next(), mx.next()
            if g == 0:
                mb_ready[b] = ts(dve, mb[:, :], mask8[:, b * S:(b + 1) * S], 1.0, BIG, ALU.subtract, ALU.mult, sem("dve_mb"))
            for h in range(2):
                bk = SB.next()
                pe.wait(k_ready[b, g], state["q"], *bk.free)
                t = mm3(bk.t[0:T, 0:SP], QOh[:, 2 * g + h, qs], QOl[:, 2 * g + h, qs], Kh[:, g, :], Kl[:, g, :],
                        True, True, sem("pe_s"))
                dve.wait(t, mb_ready[b], *sc.free, *m.free)
                o, a, acc = sc.t[:, h, :], bk.t[0:T, 0:S], m.t[:, 0, h:h + 1]
                t2 = dve.do(lambda e, o=o, a=a, acc=acc: e.tensor_tensor_reduce(
                    o, a, mb[:, :], 1.0, -3.0e38, ALU.add, ALU.max, acc), sem("dve_smax"))
                bk.free = [t2]
            k_free[g] = t
            dve.wait(t2)
            return sc, m, ts(dve, m.t[:, 1, :], m.t[:, 0, :], -XS, None, ALU.mult, s=sem("dve_nmx"))

        def exps(sc, m, t):
            act.wait(t)
            for h in range(2):
                t = activate(sc.t[:, h, :], sc.t[:, h, :], ACT.Exp, sem("act_exp"), bias=m.t[:, 1, h:h + 1],
                             scale=XS, accum_out=m.t[:, 2, h:h + 1])
            return t

        def normalise(sc, m, t, b):
            dve.wait(t)
            t = recip(m.t[:, 3, :], m.t[:, 2, :], sem("dve_rec"))
            pool.wait(t, c_any)
            for h in range(2):
                t = ts(pool, sc.t[:, h, :], sc.t[:, h, :], m.t[:, 3, h:h + 1], anyv[:, b:b + 1],
                       ALU.mult, ALU.mult, sem("pool_p"))
            m.free = [t]
            return sc, t

        def turn_p(p, t):
            pt = PT.next()
            pe.wait(t, *BA.free, *BB.free)
            for c, (o, n) in enumerate(CH):
                for h in range(2):
                    dst = BA.t[:, (2 * c + h) * T:(2 * c + h + 1) * T] if c < 2 else BB.t[0:n, h * T:(h + 1) * T]
                    tk = turn(dst, p.t[:, h, o:o + n], ident[0:T, 0:T], sem("pe_pt") if h == 1 and c > 0 else None)
                    if c == 1 and h == 1:
                        t_a = tk
            p.free = [tk]
            ph, pl = pt.t
            BA.free = [split(BA.t[:, 0:4 * T], ph[:, 0:2, :].rearrange("p a b -> p (a b)"),
                             pl[:, 0:2, :].rearrange("p a b -> p (a b)"), "pt", t_a, pt.free)]
            n = CH[2][1]
            BB.free = [split(BB.t[0:n, 0:2 * T], ph[0:n, 2, :], pl[0:n, 2, :], "pt", tk)]
            return pt, BB.free[0]

        def weighted(b, g, pt, t):
            ph, pl = pt.t
            gs = slice(g * 128, (g + 1) * 128)
            pe.wait(t, v_ready[b, g // 4], *OB.free)
            for c, (_, n) in enumerate(CH):
                tk = mm3(OB.t[:, 0:2 * T], Vh[0:n, c, gs], Vl[0:n, c, gs], ph[0:n, c, :], pl[0:n, c, :],
                         c == 0, c == 2, sem("pe_o"))
            pt.free = [tk]
            v_free[g // 4] = [tk]
            qs = slice((b - b0) * T, (b - b0 + 1) * T)
            src = OB.t[:, 0:2 * T].rearrange("p (h q) -> p h q", h=2)
            OB.free = [split(src, QOh[:, 2 * g:2 * g + 2, qs], QOl[:, 2 * g:2 * g + 2, qs], "o", tk)]
            return tk, OB.free[0]

        for g in range(3):
            project_k(b0, g)
        steps = [(b, g) for b in range(b0, b0 + HB) for g in range(NKV)]
        soft, turned = {}, {}
        last = b0 + HB - 1
        for i in range(len(steps) + 3):
            live = i < len(steps)
            if live:
                b, g = steps[i]
                sc, m, t = scores(b, g)
            if 1 <= i <= len(steps):
                soft[i - 1] = normalise(*soft[i - 1])
            if 2 <= i <= len(steps) + 1:
                turned[i - 2] = turn_p(*soft.pop(i - 2))
            if live:
                soft[i] = sc, m, exps(sc, m, t), b
                if i + 3 < len(steps):
                    project_k(*steps[i + 3])
                if b == b0 and g < 3:
                    project_v(b, 0, g)
                if 3 <= g <= 5:
                    project_v(b, 1, g - 3)
                if g == 1 and b > b0:
                    project_v(b, 0, 2)
            if i >= 3:
                done = steps[i - 3]
                state["o_pe"], state["o", done[1]] = weighted(*done, *turned.pop(i - 3))
            if live:
                if b < last and g >= 6:
                    project_v(b + 1, 0, g - 6)
                if g == 5 and b + 2 <= last:
                    ctx_turn(b + 2)
                    if b + 3 <= last:
                        ctx_load(b + 3)
                if i == len(steps) - 5:
                    xs.fill()
            if i >= len(steps) - 1:
                wo_unit(0, i - len(steps) + 1)

    def out_projection(half):
        act.wait(state["o_pe"])
        dve.wait(state["o_pe"])
        if half == 0:
            load_x(1, [act])
            state["qo_free"] = []
        xr = dma(act, XR[:, :, :], xin[:, half * HB:(half + 1) * HB, :], sem("dma_xr"))
        for u in range(1, 4):
            for f in range(KD):
                bk, t = wo_unit(u, f)
                if u == 3:
                    act.wait(t, *state.get("yt_free", []))
                    y = activate(YT[:, f, :], bk.t[:, 0:HT], ACT.Copy, sem("act_yt"))
                    bk.free = [y]
                yield
        state["qo_free"] = [t]
        state["y"], state["xr"] = y, xr

    def residual(half, rows, turn_rows):
        held = {}
        for i in range(HB):
            b, bk = half * HB + i, banks[6 + i % 2]
            state["yt_pe"] = to_rows(YT, i, bk, state["y"])
            dve.wait(state["yt_pe"], state["xr"], c_tanh, c_caus)
            x_tok = stt(XR[:, i, :], bk.t[0:T, :], tgx[:, 0:1], XR[:, i, :], ALU.mult, ALU.add, sem("dve_x1"))
            bk.free = [x_tok]
            t = stats(XR[:, i, :], mv, b, [x_tok])
            if i >= 2 and held:
                turn_rows(half, i - 2, *held.pop(i - 2))
            yield
            t = root(b, t)
            act.wait(x_tok)
            done_x1.append(dma(act, s_x1[b], XR[:, i, :], sem("dma_x1")))
            z_tok = layernorm(Z[:, b, :], XR[:, i, :], b, t)
            t = stt(ms[:, b:b + 1], mv[:, b, 1:2], rs[:, b:b + 1], rs[:, b:b + 1], ALU.mult, ALU.mult, sem("dve_ms"))
            yield
            z_ready[b] = root_square(b, t)
            act.wait(z_tok)
            if rows:
                held[i] = rows(half, i)
        for i in sorted(held):
            yield
            turn_rows(half, i, *held[i])
        state["yt_free"] = [state["yt_pe"]]

    def drain(gen, n=10 ** 6):
        for _ in range(n):
            if next(gen, gen) is gen:
                return

    for ct in CTh + CTl:
        z = ct[:, :, S:SP]
        state["pad"] = pool.do(lambda e, z=z: e.memset(f32(z), 0.0), sem("pool_pad"))
    pe.wait(state["pad"])
    nx = norm_x(0)
    drain(nx, 2)
    xs.fill()
    drain(nx)
    ctx_load(0)
    q = project_q(0)
    drain(q, 2)
    c_all = load_constants()
    for c in range(8):
        load_kv(c)
        drain(q, 1)
        if c in (3, 6):
            ctx_turn(c // 4)
            ctx_load(c // 4 + 1)
    pool.wait(c_all, c_ident)
    copy(pool, causb[:, 0, :], Z[:, 0, 0:T], sem("pool_cb"))
    c_caus = copy(pool, identb[:, :], ident[0:T, 0:T], sem("pool_cb"))
    dve.wait(c_all)
    for b in range(B):
        c_any = reduce(anyv[:, b:b + 1], mask8[:, b * S:(b + 1) * S], ALU.max, sem("dve_any"))
        if b % 2:
            drain(q, 1)
    drain(q)
    act.wait(c_all)
    activate(tgx[:, :], gx[:, :], ACT.Tanh, sem("act_tanh"))
    c_tanh = activate(tgf[:, :], gf[:, :], ACT.Tanh, sem("act_tanh"))
    attention(0)

    o = out_projection(0)
    drain(o, 1)
    nx = norm_x(1)
    for _ in range(HB + 2):
        drain(nx, 1)
        drain(o, 2)
    drain(o)
    drain(nx)
    ctx_load(4)
    q, res = project_q(1), residual(0, None, None)
    for _ in range(2 * HB):
        drain(q, 1)
        drain(res, 1)
    drain(res)
    ctx_turn(4)
    ctx_load(5)
    drain(q, 4)
    ctx_turn(5)
    ctx_load(6)
    drain(q)
    for q_ in (act, dve, pool):
        q_.wait(state["yt_free"][0], done_x1[-1])
    attention(1)

    qk_src = [[(whole, kpn(w)[:, :, m * 128:(m + 1) * 128])] for w in (wq, wk) for m in range(KD)]
    v_src = [[(flat_cols, wv[k * 128:(k + 1) * 128, :])] for k in range(KD)]
    wo_src = [[(whole, kpn(wo)[:, :, m * 128:(m + 1) * 128])] for m in range(KD)]
    dflat = w_down.rearrange("e i h -> (e i) h")

    def segments(grp, j):
        if grp == 0:
            return [(0, 128, NE, j * 128)]
        lo = (grp - 1) * 4 * EI + j * 128
        at, out_ = lo, []
        while at < lo + 128:
            e = at // EI
            end = min(lo + 128, (e + 1) * EI)
            out_.append((at - lo, end - at, e, at - e * EI))
            at = end
        return out_

    def up_units(grp, j):
        if grp == 0:
            return [[(whole, kpn(w)[:, :, j * 128:(j + 1) * 128])] for w in (sh_gate, sh_up)]
        return [[(part(o, n), kpn(w[e])[:, :, a:a + n]) for o, n, e, a in segments(grp, j)] for w in (w_gate, w_up)]

    def down_units(grp, f):
        base = sh_down if grp == 0 else dflat[(grp - 1) * 4 * EI:grp * 4 * EI, :]
        v = base.rearrange("(j p) f -> p j f", p=128)[:, :, f * 128:(f + 1) * 128]
        return [[((lambda t, n=n: t[:, 0:n, :]), v[:, a:a + n, :])] for a, n in ((0, 4), (4, 4), (8, 3))]

    N0 = 1
    s_up = [up_units(0, j) for j in range(NJ)]
    s_down = [u for f in range(KD) for u in down_units(0, f)]

    def flat(units):
        return [u for pair in units for u in pair]

    f_src = qk_src + v_src + qk_src + v_src + wo_src
    f_src += flat(s_up[:N0]) + wo_src + flat(s_up[N0:]) + s_down + flat(s_up) + s_down
    for grp in (1, 2):
        f_src += flat([up_units(grp, j) for j in range(NJ)])
        f_src += [u for f in range(KD) for u in down_units(grp, f)] * grp
    fs = Stream(fring, f_src, 4)
    n_up, n_all = 28, len(f_src) - 2 * 2 * NJ - 3 * len(s_down)
    fs.on_dve = lambda n: n_up <= n < n_all and n % 3 == 0
    DB = Ring(banks[5:8])
    ht_ready, qk_ready, v_tok, cx_ready, h2_ready = [[]] * 2, [None] * 2, [None] * 2, [None] * 2, [None] * 2

    def feature_rows(half, i):
        b = half * HB + i
        return rms_rows(b, ln1b[:, :], [z_ready[b], state["ln1"]])

    def feature_turn(half, i, h, t):
        p, t = to_features(h.t, banks[4 + i % 2], HTh[half], HTl[half], i, t, "ht")
        h.free = [p]
        ht_ready[half] = [t]

    def by_batch(ap):
        return ap.rearrange("p (b t) -> p b t", t=T)

    def project_qk(h, MB):
        for n in range(8):
            w, ready = fs.next()
            dst, bias = (QT[h], bqc) if n < 4 else (KT[h], bkc)
            m, bk = n % 4, MB.next()
            pe.wait(ready, *ht_ready[h], *bk.free)
            for k in range(KD):
                t = mm3(bk.t[:, 0:HT], w.t[:, 0, k, :], w.t[:, 1, k, :], HTh[h][:, k, :], HTl[h][:, k, :],
                        k == 0, k == KD - 1, sem("pe_qk"))
            w.free = [t]
            p = PQ.next()
            act.wait(t, *p.free)
            t2 = activate(p.t[:, 0, :], bk.t[:, 0:HT], ACT.Identity, sem("act_f"), bias=bias[:, m:m + 1])
            bk.free = [t2]
            yield
            dve.wait(t2)
            o, a = p.t[:, 1, :], p.t[:, 0, :]
            t3 = dve.do(lambda e, o=o, a=a: e.stream_shuffle(o, a, SWAP), sem("dve_shuf"))
            pool.wait(t2)
            cos4 = cosT[:, :, :].broadcast_to([128, HB, T])
            sin4 = sinT[:, :, :].broadcast_to([128, HB, T])
            t4 = tt(pool, by_batch(p.t[:, 2, :]), by_batch(p.t[:, 0, :]), cos4, ALU.mult, sem("pool_cos"))
            dve.wait(t3)
            t5 = tt(dve, by_batch(p.t[:, 1, :]), by_batch(p.t[:, 1, :]), sin4, ALU.mult, sem("dve_sin"))
            dve.wait(t4, t5)
            qk_ready[h] = tt(dve, dst[:, m, :], p.t[:, 1, :], p.t[:, 2, :], ALU.add, sem("dve_rope"))
            p.free = [qk_ready[h]]
            yield
        state["qk_pe", h] = t

    def project_v_rows(h):
        for k in range(KD):
            w, ready = fs.next()
            wh, wl = (w.t[:, a, :, :].rearrange("p a b -> p (a b)") for a in (0, 1))
            for i in range(HB):
                bk = banks[i]
                pe.wait(ready, *ht_ready[h], *bk.free)
                ts_ = slice(i * T, (i + 1) * T)
                t = mm3(bk.t[0:T, :], HTh[h][:, k, ts_], HTl[h][:, k, ts_], wh, wl, k == 0, k == KD - 1, sem("pe_fv"), True)
                if k == KD - 1:
                    dve.wait(t, state["c2"])
                    v_tok[h] = tt(dve, V[h][:, i, :], bk.t[0:T, :], bvb[:, :], ALU.add, sem("dve_v2"))
                    bk.free = [v_tok[h]]
            w.free = [t]
            yield

    def project_v_batches(h):
        units = fs.take(KD)
        for i in range(HB):
            bk, ts_ = DB.next(), slice(i * T, (i + 1) * T)
            pe.wait(*ht_ready[h], *bk.free)
            for k, (w, ready) in enumerate(units):
                pe.wait(ready)
                wh, wl = (w.t[:, a, :, :].rearrange("p a b -> p (a b)") for a in (0, 1))
                t = mm3(bk.t[0:T, :], HTh[h][:, k, ts_], HTl[h][:, k, ts_], wh, wl, k == 0, k == KD - 1, sem("pe_fv"))
            if i in (0, 1):
                fs.fetch()
            yield
            dve.wait(t, state["c2"])
            v_tok[h] = tt(dve, V[h][:, i, :], bk.t[0:T, :], bvb[:, :], ALU.add, sem("dve_v2"))
            bk.free = [v_tok[h]]
        for w, _ in units:
            w.free = [t]
        fs.fill()

    def self_attention():
        FB, TB, bko = Ring(banks[0:3]), Ring(banks[3:4]), banks[4]

        def f_scores(h, b, i):
            bs, ps = slice(b * T, (b + 1) * T), slice(32 * i, 32 * i + 32)
            p, m, bk = PF.next(), sm.next(), FB.next()
            pe.wait(qk_ready[h], c_caus, *bk.free)
            matmul(by_batch(bk.t[0:T, 0:4 * T]), identb[:, :], causb[:, :, :].broadcast_to([T, 4, T]), True, False)
            for c in range(4):
                t = matmul(bk.t[0:T, c * T:(c + 1) * T], QT[h][ps, c, bs], KT[h][ps, c, bs], False, c == 3,
                           sem("pe_fs") if c == 3 else None)
            return p, m, bk, t

        def f_max(p, m, bk, t):
            dve.wait(t, *m.free)
            t = reduce(m.t[:, 0, :], bk.t[0:T, 0:4 * T].rearrange("p (a b) -> p a b", a=4), ALU.max, sem("dve_fm"))
            dve.wait(t)
            t = ts(dve, m.t[:, 1, :], m.t[:, 0, :], -FS, None, ALU.mult, s=sem("dve_fn"))
            return p, m, bk, t

        def f_exps(p, m, bk, t):
            act.wait(t, *p.free)
            for c in range(4):
                t = activate(p.t[:, c, :], bk.t[0:T, c * T:(c + 1) * T], ACT.Exp,
                             sem("act_fe") if c == 3 else None, bias=m.t[:, 1, c:c + 1], scale=FS,
                             accum_out=m.t[:, 2, c:c + 1])
            bk.free = [t]
            return p, m, t

        def f_norm(p, m, t):
            dve.wait(t)
            t = recip(m.t[:, 3, :], m.t[:, 2, :], sem("dve_fr"))
            pool.wait(t)
            r4 = m.t[:, 3, :].rearrange("p (a o) -> p a o", o=1).broadcast_to([T, 4, T])
            t = tt(pool, p.t[:, :, :], p.t[:, :, :], r4, ALU.mult, sem("pool_fp"))
            m.free = [t]
            return p, t

        def f_turn(i, p, t):
            pt, bk = PTf.next(), TB.next()
            pe.wait(t, *bk.free)
            for c in range(4):
                tk = turn(bk.t[0:T, c * T:(c + 1) * T], p.t[:, c, :], ident[0:T, 0:T], sem("pe_ft") if c == 3 else None)
            p.free = [tk]
            dst = pt.t[:, :, :].rearrange("p a b -> p (a b)")
            if i % 2:
                dve.wait(tk, *pt.free)
                t = copy(dve, dst, bk.t[0:T, 0:4 * T], sem("dve_ft"))
            else:
                act.wait(tk, *pt.free)
                t = activate(dst, bk.t[0:T, 0:4 * T], ACT.Copy, sem("act_ft"))
            bk.free = [t]
            return pt, t

        def f_out(h, b, i, pt, t):
            bk = bko
            pe.wait(t, v_tok[h], *bk.free)
            for c in range(4):
                hcol = (4 * c + i) * FD
                t = matmul(bk.t[32 * i:32 * i + 32, c * T:(c + 1) * T], V[h][:, b, hcol:hcol + FD],
                           pt.t[:, c, :], True, True, sem("pe_fo") if c == 3 else None)
            pt.free = [t]
            if i == 3:
                bs = slice(b * T, (b + 1) * T)
                src = bk.t[:, 0:4 * T].rearrange("p (a b) -> p a b", a=4)
                cx_ready[h] = split(src, CXh[h][:, :, bs], CXl[h][:, :, bs], "cx", t)
                bk.free = [cx_ready[h]]

        units = [(h, b, i) for h in range(2) for b in range(HB) for i in range(4)]
        raised, normed, turned = {}, {}, {}
        for n in range(len(units) + 4):
            live = n < len(units)
            ahead = n + 1 < len(units)
            if n == 0:
                scored = f_max(*f_scores(*units[0]))
            if ahead:
                banked = f_scores(*units[n + 1])
            if 3 <= n <= len(units) + 2:
                turned[n - 3] = f_turn(units[n - 3][2], *normed.pop(n - 3))
            if n >= 4:
                f_out(*units[n - 4], *turned.pop(n - 4))
            if live:
                raised[n] = f_exps(*scored)
            if 1 <= n <= len(units):
                normed[n - 1] = f_norm(*raised.pop(n - 1))
            if ahead:
                scored = f_max(*banked)
            yield

    def project_o(h):
        for m in range(KD):
            w, ready = fs.next()
            bk = DB.next()
            pe.wait(ready, cx_ready[h], *bk.free)
            for k in range(KD):
                t = mm3(bk.t[:, 0:HT], w.t[:, 0, k, :], w.t[:, 1, k, :], CXh[h][:, k, :], CXl[h][:, k, :],
                        k == 0, k == KD - 1, sem("pe_fo2"))
            w.free = [t]
            act.wait(t, *state["yt_free"])
            y = activate(YTf[:, m, :], bk.t[:, 0:HT], ACT.Copy, sem("act_yt"))
            bk.free = [y]
            yield
        state["y"], state["wo_pe", h] = y, t

    def epilogue(h):
        for q in (act, dve):
            q.wait(state["qk_pe", 1])
        b0 = h * HB
        for i in range(HB):
            b, bk = b0 + i, DB.next()
            t = to_rows(YTf, i, bk, state["y"])
            dve.wait(t)
            state["yt_free"] = [t]
            t = tt(dve, Z[:, b, :], bk.t[0:T, :], Z[:, b, :], ALU.add, sem("dve_x2"))
            bk.free = [t]
            t = mean_square(b, [t])
            yield
        act.wait(t)
        t = activate(rz[:, b0:b0 + HB], ms[:, b0:b0 + HB], ACT.Sqrt, sem("act_sqrt"), bias=eps2[:, 0:1])
        dve.wait(t)
        inv = recip(rz[:, b0:b0 + HB], rz[:, b0:b0 + HB], sem("dve_rs"))
        held = [rms_rows(b0 + i, ln2b[:, :], [inv, state["c2"]], False) for i in range(2)]
        yield
        for i in range(HB):
            hr, t = held.pop(0)
            if i + 2 < HB:
                held.append(rms_rows(b0 + i + 2, ln2b[:, :], [inv, state["c2"]], False))
            p, h2_ready[h] = to_features(hr.t, DB.next(), H2h[h], H2l[h], i, t, "h2")
            hr.free = [p]
            yield
        bk = DB.next()
        pe.wait(h2_ready[h], state["wr"], *bk.free)
        for k in range(KD):
            t = mm3(bk.t[0:10, 0:HT], WRh[:, k, :], WRl[:, k, :], H2h[h][:, k, :], H2l[h][:, k, :],
                    k == 0, k == KD - 1, sem("pe_r"))
        act.wait(t)
        t = activate(LT[:, :], bk.t[0:10, 0:HT], ACT.Copy, sem("act_r"))
        bk.free = [t]
        yield
        bk = DB.next()
        pe.wait(t, *bk.free)
        for i in range(HB):
            t = turn(bk.t[0:T, i * 10:i * 10 + 10], LT[:, i * T:(i + 1) * T], ident[0:10, 0:10],
                     sem("pe_turn") if i == HB - 1 else None)
        sd = sem("dve_r")

        def link(t):
            dve.wait(t)

        def wide(i):
            return r1[:, i, :].rearrange("p (b o) -> p b o", o=1).broadcast_to([T, HB, NE])

        dve.wait(t, state["io"], *state.get("comb_free", []))
        t = copy(dve, L[:, :, :], bk.t[0:T, 0:HB * 10].rearrange("p (b n) -> p b n", n=10), sd)
        bk.free = [t]
        link(t)
        link(reduce(r1[:, 0, :], L[:, :, 0:NE], ALU.max, sd))
        t = tt(dve, pr[:, :, :], L[:, :, 0:NE], wide(0), ALU.subtract, sd)
        act.wait(t)
        t = activate(pr[:, :, :], pr[:, :, :], ACT.Exp, sem("act_r"))
        sg = activate(L[:, :, NE:NE + 1], L[:, :, NE:NE + 1], ACT.Tanh, sem("act_r"), scale=0.5)
        yield
        link(t)
        link(reduce(r1[:, 0, :], pr[:, :, :], ALU.add, sd))
        link(recip(r1[:, 1, :], r1[:, 0, :], sd))
        link(tt(dve, pr[:, :, :], pr[:, :, :], wide(1), ALU.mult, sd))
        src = pr
        for r, sl in ((0, sel1), (1, sel2)):
            link(reduce(r1[:, 2, :], src[:, :, :], ALU.max, sd))
            link(tt(dve, sl[:, :, :], src[:, :, :], wide(2), ALU.is_equal, sd))
            link(tt(dve, sl[:, :, :], sl[:, :, :], io8[:, :, :], ALU.mult, sd))
            link(reduce(r1[:, 3, :], sl[:, :, :], ALU.max, sd))
            link(tt(dve, sl[:, :, :], io8[:, :, :], wide(3), ALU.is_equal, sd))
            if r == 0:
                link(stt(w8[:, :, :], sl[:, :, :], -4.0, pr[:, :, :], ALU.mult, ALU.add, sd))
                src = w8
                yield
        link(tt(dve, sel1[:, :, :], sel1[:, :, :], sel2[:, :, :], ALU.add, sd))
        stt(comb[:, :, 0:NE], pr[:, :, :], 0.5, sel1[:, :, :], ALU.mult, ALU.mult, sd)
        dve.wait(sg)
        t = ts(dve, comb[:, :, NE:NE + 1], L[:, :, NE:NE + 1], 0.25, 0.25, ALU.mult, ALU.add, s=sd)
        yield
        bk = DB.next()
        pe.wait(t, *bk.free)
        for i in range(HB):
            tk = turn(bk.t[0:NE + 1, i * T:(i + 1) * T], comb[:, i, :], ident[0:T, 0:T],
                      sem("pe_turn") if i == HB - 1 else None)
        dve.wait(tk)
        ct = copy(dve, combT[:, :], bk.t[0:NE + 1, 0:HT], sem("dve_ct2"))
        bk.free = [ct]
        act.wait(ct)
        state["comb", h] = dma(act, s_comb[h], combT[:, :], sem("dma_comb"))
        state["comb_free"] = [state["comb", h]]

    hd_free, hd_ready, y_ready = [[], []], [{}, {}], [None, None]

    gates = {}

    def load_gates(grp, j, h):
        if j < NJ and (grp, j, h) not in gates:
            gt = G.next()
            sp.wait(state["comb", h], *gt.free)
            for o, n, e, _ in segments(grp, j):
                t = dma(sp, gt.t[o:o + n, :], bass.AP(s_comb.tensor, (h * (NE + 1) + e) * HT, [[0, n], [1, HT]]), gt.sem)
            gates[grp, j, h] = gt, t

    def up(grp, j, halves, MB):
        tms = []

        def tile(w, ready, h, bk):
            pe.wait(ready, h2_ready[h], *bk.free)
            for k in range(KD):
                t = mm3(bk.t[:, 0:HT], w.t[:, 0, k, :], w.t[:, 1, k, :], H2h[h][:, k, :], H2l[h][:, k, :],
                        k == 0, k == KD - 1, sem("pe_gu"))
            return t

        w, ready = fs.next()
        for h in halves:
            bk, tm = MB.next(), TM.next()
            t = tile(w, ready, h, bk)
            act.wait(t, *tm.free)
            s_tok = activate(tm.t[:, 0, :], bk.t[:, 0:HT], ACT.Tanh, sem("act_th"), scale=0.5)
            dve.wait(s_tok)
            tok = stt(tm.t[:, 0, :], tm.t[:, 0, :], 1.0, bk.t[:, 0:HT], ALU.add, ALU.mult, sem("dve_silu"))
            bk.free = [tok]
            tms.append((tm, tok))
        w.free = [t]
        late = halves == [0] and j == N0
        if not late:
            weigh()
        yield
        w, ready = fs.next()
        if late:
            weigh()
        for h, (tm, tok) in zip(halves, tms):
            bk = MB.next()
            t = tile(w, ready, h, bk)
            dve.wait(t, tok)
            m_tok = tt(dve, tm.t[:, 0, :], bk.t[:, 0:HT], tm.t[:, 0, :], ALU.mult, sem("dve_gu"))
            bk.free = [m_tok]
            unweighed.append((grp, j, h, tm, m_tok))
        w.free = [t]
        if len(halves) == 2:
            weigh()
        yield

    unweighed = []

    def weigh():
        for grp, j, h, _, _ in unweighed:
            load_gates(grp, j, h)
        for grp, j, h, _, _ in unweighed:
            load_gates(grp, j + 1, h)
        for grp, j, h, tm, m_tok in unweighed:
            gt, g_tok = gates.pop((grp, j, h))
            pool.wait(m_tok, g_tok)
            p_tok = tt(pool, tm.t[:, 1, :], tm.t[:, 0, :], gt.t[:, :], ALU.mult, sem("pool_gu"))
            gt.free = [p_tok]
            act.wait(p_tok, *hd_free[h])
            h_tok = activate(HDh[h][:, j, :], tm.t[:, 1, :], ACT.Copy, sem("act_hd"))
            dve.wait(h_tok)
            hd_tok = tt(dve, HDl[h][:, j, :], tm.t[:, 1, :], f32(HDh[h][:, j, :]), ALU.subtract, sem("dve_hd"))
            tm.free = [hd_tok]
            hd_ready[h][j] = [h_tok, hd_tok]
        unweighed.clear()

    def down(grp, halves, MB):
        weigh()
        for f in range(KD):
            bks = [MB.next() for _ in halves]
            for a, n in ((0, 4), (4, 4), (8, 3)):
                w, ready = fs.next()
                for h, bk in zip(halves, bks):
                    pe.wait(ready, *bk.free)
                    for jj in range(n):
                        j = a + jj
                        pe.wait(*hd_ready[h][j])
                        t = mm3(bk.t[:, 0:HT], w.t[:, 0, jj, :], w.t[:, 1, jj, :], HDh[h][:, j, :], HDl[h][:, j, :],
                                j == 0, j == NJ - 1, sem("pe_d"), jj == n - 1)
                    if a == 8:
                        if grp == 0:
                            act.wait(t, *state["y_free"])
                            y_ready[h] = activate(Y[h][:, f, :], bk.t[:, 0:HT], ACT.Copy, sem("act_y"))
                        else:
                            dve.wait(t, y_ready[h])
                            y_ready[h] = tt(dve, Y[h][:, f, :], bk.t[:, 0:HT], Y[h][:, f, :], ALU.add, sem("dve_y"))
                        bk.free = [y_ready[h]]
                w.free = [t]
                yield
        for h in halves:
            hd_free[h] = [t]

    act.wait(state["o_pe"])
    dve.wait(state["o_pe"])
    pool.wait(state["o_pe"])
    state["ln1"] = dma(act, ln1b[:, :], bass.AP(w_ln1.tensor, 0, [[0, T], [1, D]]), sem("dma_ln1"))

    o = out_projection(1)
    drain(o, 1)
    fs.fill()
    rows = feature_rows(0, 0)
    for i in range(HB):
        drain(o, 3)
        feature_turn(0, i, *rows)
        if i + 1 < HB:
            rows = feature_rows(0, i + 1)
    drain(o)
    wo_done = state["qo_free"][0]
    for q in (act, dve, pool):
        q.wait(wo_done)
    dma(act, bvb[:, :], bass.AP(b_v.tensor, 0, [[0, T], [1, D]]), sem("dma_c2"))
    state["c2"] = dma(act, ln2b[:, :], bass.AP(w_ln2.tensor, 0, [[0, T], [1, D]]), sem("dma_c2"))
    z_tok = pool.do(lambda e: e.memset(WR[:, :, :], 0.0), sem("pool_wr"))
    for i in range(NE):
        zi = io8[:, :, i:i + 1]
        state["io"] = pool.do(lambda e, zi=zi, i=i: e.memset(zi, float(NE - i)), sem("pool_wr"))
    act.wait(z_tok)
    dma(act, WR[:, :, 0:NE], kpn(w_router), sem("dma_wr"))
    wt = dma_columns(act, WR[:, :, NE:NE + 1], kpn(sh_eg), sem("dma_wr"))

    dense = chain(project_qk(0, Ring(banks[0:4])), project_v_rows(0))
    res = residual(1, feature_rows, feature_turn)
    drain(dense, 1)
    for n in range(2 * HB + 2):
        drain(dense, 1 if n == 8 else 2)
        drain(res, 1)
    drain(res)
    pool.wait(wt)
    h = copy(pool, WRh[:, :, :], WR[:, :, :], sem("pool_wr"))
    pool.wait(h)
    state["wr"] = tt(pool, WRl[:, :, :], WR[:, :, :], f32(WRh[:, :, :]), ALU.subtract, sem("pool_wr"))
    drain(dense)
    qk, at = project_qk(1, DB), self_attention()
    drain(at, 1)
    drain(qk, 1)
    for n in range(12):
        drain(at, 1)
        drain(qk, 2 if n < 3 else 1)
    drain(qk)
    v = project_v_batches(1)
    for _ in range(5):
        drain(at, 1)
        drain(v, 1)
    drain(at, 2)
    o, ep = project_o(0), epilogue(0)
    for _ in range(4):
        drain(o, 1)
        drain(at, 1)
    drain(o)
    for _ in range(9):
        drain(ep, 1)
        drain(at, 1)
    for q in (act, dve, pool):
        q.wait(state["wo_pe", 0], qk_ready[1])
    state["y_free"] = [done_x1[-1]]

    def shared(h, MB, js):
        for j in js:
            yield from up(0, j, [h], MB)

    s0, o = shared(0, DB, range(N0)), project_o(1)
    drain(ep, 1)
    drain(s0, 1)
    drain(at)
    drain(ep, 1)
    drain(s0)
    drain(ep, 1)
    drain(o, 2)
    drain(ep, 1)
    drain(o)
    drain(ep)
    s0, ep = shared(0, DB, range(N0, NJ)), epilogue(1)
    for _ in range(9):
        drain(ep, 1)
        drain(s0, 1)
    s1 = chain(s0, down(0, [0], DB))
    for n in (2, 1, 1, 2):
        drain(ep, 1)
        drain(s1, n)
    drain(ep)
    drain(s1)
    MB = Ring(banks)
    for q in (act, dve):
        q.wait(state["wo_pe", 1])
    drain(shared(1, MB, range(NJ)))
    drain(down(0, [1], MB))

    def add_x1():
        sp.wait(done_x1[-1])
        for b in range(B):
            r = HR.next()
            sp.wait(*r.free)
            t = dma(sp, r.t[:, :], s_x1[b], sem(f"dma_hr{b % 3}"))
            dve.wait(t)
            t = stt(Z[:, b, :], Z[:, b, :], tgf[:, 0:1], r.t[:, :], ALU.mult, ALU.add, sem("dve_zf"))
            r.free = [t]
            yield
        state["zf"] = t

    def result(h, i):
        b, bk, o = h * HB + i, MB.next(), OUT.next()
        t = to_rows(Y[h], i, bk, y_ready[h])
        dve.wait(t, state["zf"], *o.free)
        t = stt(o.t[:, :], bk.t[0:T, :], tgf[:, 0:1], Z[:, b, :], ALU.mult, ALU.add, sem("dve_out"))
        bk.free = [t]
        act.wait(t)
        o.free = [dma(act, out[b], o.t[:, :], o.sem)]

    zf = add_x1()
    for grp in (1, 2):
        for j in range(NJ):
            drain(up(grp, j, [0, 1], MB))
            drain(zf, 1)
        if grp == 1:
            drain(zf)
            drain(down(1, [0, 1], MB))
    drain(down(2, [0], MB))
    d1 = down(2, [1], MB)
    drain(d1, 1)
    for i in range(HB):
        result(0, i)
        drain(d1, 1)
    drain(d1)
    for i in range(HB):
        result(1, i)
    act.wait(*[tok for o in OUT.slots for tok in o.free])
    sp.wait(*done_x1, state["comb", 0], state["comb", 1])

    with top:
        block = top.enter_context(nc.Block())

        @block.sync
        def _(eng):
            sp.play(eng)

        @block.scalar
        def _(eng):
            act.play(eng)

        @block.vector
        def _(eng):
            dve.play(eng)

        @block.gpsimd
        def _(eng):
            pool.play(eng)

        @block.tensor
        def _(eng):
            pe.play(eng)


_INS = ['x', 'ctx_1024', 'mask_BxS2_bf1', 'g_xattn', 'g_ffn', 'L0_xattn_Wq', 'L0_xattn_Wk', 'L0_xattn_Wv',
        'L0_xattn_Wo', 'L0_ffn_w_ln1', 'L0_ffn_wq', 'L0_ffn_bq', 'L0_ffn_wk', 'L0_ffn_bk', 'L0_ffn_wv',
        'L0_ffn_bv', 'L0_ffn_wo', 'L0_ffn_w_ln2', 'L0_ffn_w_router', 'L0_ffn_w_gate_e', 'L0_ffn_w_up_e',
        'L0_ffn_w_down_e', 'L0_ffn_w_sh_gate', 'L0_ffn_w_sh_up', 'L0_ffn_w_sh_down', 'L0_ffn_w_sh_eg']


def _constants():
    ident = np.eye(128, dtype=np.float32)
    causal = np.where(np.tril(np.ones((T, T), bool)), np.float32(0), np.float32(-BIG)).astype(np.float32)
    inv = (np.float32(1.0) / np.power(np.float32(1.0e6), np.arange(0, FD, 2, dtype=np.float32) / np.float32(FD))).astype(np.float32)
    ang = (np.arange(T, dtype=np.float32)[:, None] * inv[None, :]).astype(np.float32)
    emb = np.concatenate([ang, ang], axis=-1)
    cos = np.cos(emb).astype(np.float32).T
    sin = np.sin(emb).astype(np.float32).T
    sin = np.concatenate([-sin[:FD // 2], sin[FD // 2:]], axis=0)
    return {'c_id': ident, 'c_causal': causal, 'c_cos': np.ascontiguousarray(np.tile(cos, (4, 1))),
            'c_sin': np.ascontiguousarray(np.tile(sin, (4, 1)))}


def kernel(**inputs):
    import numpy as _np
    import concourse.bacc as _bacc
    from concourse import mybir as _mybir
    from concourse.bass_utils import run_bass_kernel_spmd as _run

    nc = _bacc.Bacc("TRN2", target_bir_lowering=False, num_devices=1)
    arrays, args = {}, []
    for name in _INS:
        a = _np.ascontiguousarray(inputs[name])
        if a.dtype == _np.bool_:
            a = a.view(_np.uint8)
        arrays[f"in_{name}_dram"] = a
        args.append(nc.dram_tensor(f"in_{name}_dram", a.shape, _mybir.dt.from_np(a.dtype), kind="ExternalInput").ap())
    for name, a in _constants().items():
        arrays[f"in_{name}_dram"] = a
        args.append(nc.dram_tensor(f"in_{name}_dram", a.shape, _mybir.dt.from_np(a.dtype), kind="ExternalInput").ap())
    for name, shape in (("s_x1", (B, T, D)), ("s_comb", (2, NE + 1, HT))):
        args.append(nc.dram_tensor(name, shape, F, kind="Internal").ap())
    args.append(nc.dram_tensor("out_0_dram", (B, T, D), F, kind="ExternalOutput").ap())
    flamingo_kernel(nc, *args)
    r = _run(nc, [arrays], core_ids=[0])
    return r.results[0]["out_0_dram"]
```
